# Optimizing a Trainium2 kernel written in Bass

```python
import numpy as np
import jax
import jax.numpy as jnp

def _softmax(x, axis=-1):
    return jax.nn.softmax(x, axis=axis)

def _gelu(x):
    return jax.nn.gelu(x, approximate=True)

def _silu(x):
    return jax.nn.silu(x)

def _sigmoid(x):
    return jax.nn.sigmoid(x)

def _layernorm(x, axis=-1, eps=1e-05):
    m = jnp.mean(x, axis=axis, keepdims=True)
    v = jnp.var(x, axis=axis, keepdims=True)
    return (x - m) / jnp.sqrt(v + eps)

def _scatter_add(tgt, idx, src, axis=0):
    return tgt.at[idx].add(src)

def _segment_sum(src, seg, n):
    return jax.ops.segment_sum(src, seg, n)
kernel_name = 'mk_dlrm_tower_d1_rec_r8_1dddff'

def setup_inputs(seed: int=0):
    np.random.seed(seed)
    _w = jnp.asarray

    def _rec_inputs():
        import jax
        import jax.numpy as jnp
        _tk = jax.random.key(seed)
        dense_ctx = jax.random.normal(jax.random.fold_in(_tk, 190), (512, 16), jnp.float32)
        ids = jnp.stack([jax.random.randint(jax.random.fold_in(_tk, 200 + f), (512,), 0, v, jnp.int32) for f, v in enumerate([1250, 12500, 1250, 1250, 1000, 1000, 1250, 12500, 12500, 1250, 1000, 1250, 12500, 1000, 1250, 1250, 1250, 1250, 1250, 12500, 1000, 1000, 1250, 1250, 1000, 1000, 1250, 12500, 1250, 1000, 1000, 1000, 1000, 1000, 1250, 1000, 1000, 1250, 1000, 1250, 1000, 1000, 1000, 1250, 1250, 1250, 1000, 1000, 1000, 1000])], axis=1)
        tbl_0 = 0.05 * jax.random.normal(jax.random.fold_in(_tk, 500 + 0), (1250, 300), jnp.float32)
        tbl_1 = 0.05 * jax.random.normal(jax.random.fold_in(_tk, 500 + 1), (12500, 300), jnp.float32)
        tbl_2 = 0.05 * jax.random.normal(jax.random.fold_in(_tk, 500 + 2), (1250, 300), jnp.float32)
        tbl_3 = 0.05 * jax.random.normal(jax.random.fold_in(_tk, 500 + 3), (1250, 300), jnp.float32)
        tbl_4 = 0.05 * jax.random.normal(jax.random.fold_in(_tk, 500 + 4), (1000, 300), jnp.float32)
        tbl_5 = 0.05 * jax.random.normal(jax.random.fold_in(_tk, 500 + 5), (1000, 300), jnp.float32)
        tbl_6 = 0.05 * jax.random.normal(jax.random.fold_in(_tk, 500 + 6), (1250, 300), jnp.float32)
        tbl_7 = 0.05 * jax.random.normal(jax.random.fold_in(_tk, 500 + 7), (12500, 300), jnp.float32)
        tbl_8 = 0.05 * jax.random.normal(jax.random.fold_in(_tk, 500 + 8), (12500, 300), jnp.float32)
        tbl_9 = 0.05 * jax.random.normal(jax.random.fold_in(_tk, 500 + 9), (1250, 300), jnp.float32)
        tbl_10 = 0.05 * jax.random.normal(jax.random.fold_in(_tk, 500 + 10), (1000, 300), jnp.float32)
        tbl_11 = 0.05 * jax.random.normal(jax.random.fold_in(_tk, 500 + 11), (1250, 300), jnp.float32)
        tbl_12 = 0.05 * jax.random.normal(jax.random.fold_in(_tk, 500 + 12), (12500, 300), jnp.float32)
        tbl_13 = 0.05 * jax.random.normal(jax.random.fold_in(_tk, 500 + 13), (1000, 300), jnp.float32)
        tbl_14 = 0.05 * jax.random.normal(jax.random.fold_in(_tk, 500 + 14), (1250, 300), jnp.float32)
        tbl_15 = 0.05 * jax.random.normal(jax.random.fold_in(_tk, 500 + 15), (1250, 300), jnp.float32)
        tbl_16 = 0.05 * jax.random.normal(jax.random.fold_in(_tk, 500 + 16), (1250, 300), jnp.float32)
        tbl_17 = 0.05 * jax.random.normal(jax.random.fold_in(_tk, 500 + 17), (1250, 300), jnp.float32)
        tbl_18 = 0.05 * jax.random.normal(jax.random.fold_in(_tk, 500 + 18), (1250, 300), jnp.float32)
        tbl_19 = 0.05 * jax.random.normal(jax.random.fold_in(_tk, 500 + 19), (12500, 300), jnp.float32)
        tbl_20 = 0.05 * jax.random.normal(jax.random.fold_in(_tk, 500 + 20), (1000, 300), jnp.float32)
        tbl_21 = 0.05 * jax.random.normal(jax.random.fold_in(_tk, 500 + 21), (1000, 300), jnp.float32)
        tbl_22 = 0.05 * jax.random.normal(jax.random.fold_in(_tk, 500 + 22), (1250, 300), jnp.float32)
        tbl_23 = 0.05 * jax.random.normal(jax.random.fold_in(_tk, 500 + 23), (1250, 300), jnp.float32)
        tbl_24 = 0.05 * jax.random.normal(jax.random.fold_in(_tk, 500 + 24), (1000, 300), jnp.float32)
        tbl_25 = 0.05 * jax.random.normal(jax.random.fold_in(_tk, 500 + 25), (1000, 300), jnp.float32)
        tbl_26 = 0.05 * jax.random.normal(jax.random.fold_in(_tk, 500 + 26), (1250, 300), jnp.float32)
        tbl_27 = 0.05 * jax.random.normal(jax.random.fold_in(_tk, 500 + 27), (12500, 300), jnp.float32)
        tbl_28 = 0.05 * jax.random.normal(jax.random.fold_in(_tk, 500 + 28), (1250, 300), jnp.float32)
        tbl_29 = 0.05 * jax.random.normal(jax.random.fold_in(_tk, 500 + 29), (1000, 300), jnp.float32)
        tbl_30 = 0.05 * jax.random.normal(jax.random.fold_in(_tk, 500 + 30), (1000, 300), jnp.float32)
        tbl_31 = 0.05 * jax.random.normal(jax.random.fold_in(_tk, 500 + 31), (1000, 300), jnp.float32)
        tbl_32 = 0.05 * jax.random.normal(jax.random.fold_in(_tk, 500 + 32), (1000, 300), jnp.float32)
        tbl_33 = 0.05 * jax.random.normal(jax.random.fold_in(_tk, 500 + 33), (1000, 300), jnp.float32)
        tbl_34 = 0.05 * jax.random.normal(jax.random.fold_in(_tk, 500 + 34), (1250, 300), jnp.float32)
        tbl_35 = 0.05 * jax.random.normal(jax.random.fold_in(_tk, 500 + 35), (1000, 300), jnp.float32)
        tbl_36 = 0.05 * jax.random.normal(jax.random.fold_in(_tk, 500 + 36), (1000, 300), jnp.float32)
        tbl_37 = 0.05 * jax.random.normal(jax.random.fold_in(_tk, 500 + 37), (1250, 300), jnp.float32)
        tbl_38 = 0.05 * jax.random.normal(jax.random.fold_in(_tk, 500 + 38), (1000, 300), jnp.float32)
        tbl_39 = 0.05 * jax.random.normal(jax.random.fold_in(_tk, 500 + 39), (1250, 300), jnp.float32)
        tbl_40 = 0.05 * jax.random.normal(jax.random.fold_in(_tk, 500 + 40), (1000, 300), jnp.float32)
        tbl_41 = 0.05 * jax.random.normal(jax.random.fold_in(_tk, 500 + 41), (1000, 300), jnp.float32)
        tbl_42 = 0.05 * jax.random.normal(jax.random.fold_in(_tk, 500 + 42), (1000, 300), jnp.float32)
        tbl_43 = 0.05 * jax.random.normal(jax.random.fold_in(_tk, 500 + 43), (1250, 300), jnp.float32)
        tbl_44 = 0.05 * jax.random.normal(jax.random.fold_in(_tk, 500 + 44), (1250, 300), jnp.float32)
        tbl_45 = 0.05 * jax.random.normal(jax.random.fold_in(_tk, 500 + 45), (1250, 300), jnp.float32)
        tbl_46 = 0.05 * jax.random.normal(jax.random.fold_in(_tk, 500 + 46), (1000, 300), jnp.float32)
        tbl_47 = 0.05 * jax.random.normal(jax.random.fold_in(_tk, 500 + 47), (1000, 300), jnp.float32)
        tbl_48 = 0.05 * jax.random.normal(jax.random.fold_in(_tk, 500 + 48), (1000, 300), jnp.float32)
        tbl_49 = 0.05 * jax.random.normal(jax.random.fold_in(_tk, 500 + 49), (1000, 300), jnp.float32)
        _rk = jax.random.fold_in(_tk, 7)
        r_label_embedding = -1.64977e-06 + 0.999867 * jax.random.normal(jax.random.fold_in(_rk, 101), (512, 200, 300), jnp.float32)
        W_top1 = 0.0680414 * jax.random.normal(jax.random.fold_in(_tk, 801), (216, 512), jnp.float32)
        W_top2 = 0.0441942 * jax.random.normal(jax.random.fold_in(_tk, 802), (512, 256), jnp.float32)
        W_top3 = 0.0625 * jax.random.normal(jax.random.fold_in(_tk, 803), (256, 1), jnp.float32)
        b_top1 = jnp.zeros((512,), jnp.float32)
        b_top2 = jnp.zeros((256,), jnp.float32)
        return (dense_ctx, ids, tbl_0, tbl_1, tbl_2, tbl_3, tbl_4, tbl_5, tbl_6, tbl_7, tbl_8, tbl_9, tbl_10, tbl_11, tbl_12, tbl_13, tbl_14, tbl_15, tbl_16, tbl_17, tbl_18, tbl_19, tbl_20, tbl_21, tbl_22, tbl_23, tbl_24, tbl_25, tbl_26, tbl_27, tbl_28, tbl_29, tbl_30, tbl_31, tbl_32, tbl_33, tbl_34, tbl_35, tbl_36, tbl_37, tbl_38, tbl_39, tbl_40, tbl_41, tbl_42, tbl_43, tbl_44, tbl_45, tbl_46, tbl_47, tbl_48, tbl_49, r_label_embedding, W_top1, b_top1, W_top2, b_top2, W_top3)
    dense_ctx, ids, tbl_0, tbl_1, tbl_2, tbl_3, tbl_4, tbl_5, tbl_6, tbl_7, tbl_8, tbl_9, tbl_10, tbl_11, tbl_12, tbl_13, tbl_14, tbl_15, tbl_16, tbl_17, tbl_18, tbl_19, tbl_20, tbl_21, tbl_22, tbl_23, tbl_24, tbl_25, tbl_26, tbl_27, tbl_28, tbl_29, tbl_30, tbl_31, tbl_32, tbl_33, tbl_34, tbl_35, tbl_36, tbl_37, tbl_38, tbl_39, tbl_40, tbl_41, tbl_42, tbl_43, tbl_44, tbl_45, tbl_46, tbl_47, tbl_48, tbl_49, r_label_embedding, W_top1, b_top1, W_top2, b_top2, W_top3 = _rec_inputs()

    def _L0_rec_setup():
        import jax, jax.numpy as jnp
        import numpy as np
        E, U, C, T, N, B, K = (300, 300, 4, 8, 50, 512, 200)
        P = E * (E - 1) // 2
        PAD = jnp.float32(-2 ** 32 + 1)

        def _attn_pool(x, mask, w_a, b_a, w_b):
            score = jnp.exp((x @ w_a + b_a) @ w_b)
            score = jnp.where(mask == 0, PAD, score)
            p = jax.nn.softmax(score, axis=1)
            return jnp.einsum('bne,bn->be', x, p[..., 0])
        key = jax.random.key(seed)
        ks = jax.random.split(key, 20)
        s = 0.02
        return {'x': jax.random.normal(ks[0], (B, N, E), jnp.float32), 'label_embedding': jax.random.normal(ks[1], (B, K, U), jnp.float32), 'w1': jax.random.normal(ks[2], (E, T), jnp.float32) * s, 'b1': jnp.zeros((T,), jnp.float32), 'w2': jax.random.normal(ks[3], (T, 1), jnp.float32) * s, 'w3': jax.random.normal(ks[4], (E, T), jnp.float32) * s, 'b3': jnp.zeros((T,), jnp.float32), 'w4': jax.random.normal(ks[5], (T, 1), jnp.float32) * s, 'w5': jax.random.normal(ks[6], (2 * E, E), jnp.float32) * s, 'b5': jnp.zeros((E,), jnp.float32), 'w6': jax.random.normal(ks[7], (E, E), jnp.float32) * s, 'b6': jnp.zeros((E,), jnp.float32), 'w7': jax.random.normal(ks[8], (P, E), jnp.float32) * s, 'b7': jnp.zeros((E,), jnp.float32), 'w8': jax.random.normal(ks[9], (2 * E, U), jnp.float32) * s, 'b8': jnp.zeros((U,), jnp.float32), 'v': jax.random.uniform(ks[10], (E, C), jnp.float32)}
    _L0_rec_all = _L0_rec_setup()
    _L0_rec_in = {k: v for k, v in _L0_rec_all.items() if k in ('w1', 'b1', 'w2', 'w3', 'b3', 'w4', 'w5', 'b5', 'w6', 'b6', 'w7', 'b7', 'w8', 'b8', 'v')}
    del _L0_rec_all
    return {'dense_ctx': dense_ctx, 'ids': ids, 'tbl_0': tbl_0, 'tbl_1': tbl_1, 'tbl_2': tbl_2, 'tbl_3': tbl_3, 'tbl_4': tbl_4, 'tbl_5': tbl_5, 'tbl_6': tbl_6, 'tbl_7': tbl_7, 'tbl_8': tbl_8, 'tbl_9': tbl_9, 'tbl_10': tbl_10, 'tbl_11': tbl_11, 'tbl_12': tbl_12, 'tbl_13': tbl_13, 'tbl_14': tbl_14, 'tbl_15': tbl_15, 'tbl_16': tbl_16, 'tbl_17': tbl_17, 'tbl_18': tbl_18, 'tbl_19': tbl_19, 'tbl_20': tbl_20, 'tbl_21': tbl_21, 'tbl_22': tbl_22, 'tbl_23': tbl_23, 'tbl_24': tbl_24, 'tbl_25': tbl_25, 'tbl_26': tbl_26, 'tbl_27': tbl_27, 'tbl_28': tbl_28, 'tbl_29': tbl_29, 'tbl_30': tbl_30, 'tbl_31': tbl_31, 'tbl_32': tbl_32, 'tbl_33': tbl_33, 'tbl_34': tbl_34, 'tbl_35': tbl_35, 'tbl_36': tbl_36, 'tbl_37': tbl_37, 'tbl_38': tbl_38, 'tbl_39': tbl_39, 'tbl_40': tbl_40, 'tbl_41': tbl_41, 'tbl_42': tbl_42, 'tbl_43': tbl_43, 'tbl_44': tbl_44, 'tbl_45': tbl_45, 'tbl_46': tbl_46, 'tbl_47': tbl_47, 'tbl_48': tbl_48, 'tbl_49': tbl_49, 'r_label_embedding': r_label_embedding, 'W_top1': W_top1, 'b_top1': b_top1, 'W_top2': W_top2, 'b_top2': b_top2, 'W_top3': W_top3, 'L0_rec_w1': _L0_rec_in['w1'], 'L0_rec_b1': _L0_rec_in['b1'], 'L0_rec_w2': _L0_rec_in['w2'], 'L0_rec_w3': _L0_rec_in['w3'], 'L0_rec_b3': _L0_rec_in['b3'], 'L0_rec_w4': _L0_rec_in['w4'], 'L0_rec_w5': _L0_rec_in['w5'], 'L0_rec_b5': _L0_rec_in['b5'], 'L0_rec_w6': _L0_rec_in['w6'], 'L0_rec_b6': _L0_rec_in['b6'], 'L0_rec_w7': _L0_rec_in['w7'], 'L0_rec_b7': _L0_rec_in['b7'], 'L0_rec_w8': _L0_rec_in['w8'], 'L0_rec_b8': _L0_rec_in['b8'], 'L0_rec_v': _L0_rec_in['v']}

def reference(dense_ctx, ids, tbl_0, tbl_1, tbl_2, tbl_3, tbl_4, tbl_5, tbl_6, tbl_7, tbl_8, tbl_9, tbl_10, tbl_11, tbl_12, tbl_13, tbl_14, tbl_15, tbl_16, tbl_17, tbl_18, tbl_19, tbl_20, tbl_21, tbl_22, tbl_23, tbl_24, tbl_25, tbl_26, tbl_27, tbl_28, tbl_29, tbl_30, tbl_31, tbl_32, tbl_33, tbl_34, tbl_35, tbl_36, tbl_37, tbl_38, tbl_39, tbl_40, tbl_41, tbl_42, tbl_43, tbl_44, tbl_45, tbl_46, tbl_47, tbl_48, tbl_49, r_label_embedding, W_top1, b_top1, W_top2, b_top2, W_top3, L0_rec_w1, L0_rec_b1, L0_rec_w2, L0_rec_w3, L0_rec_b3, L0_rec_w4, L0_rec_w5, L0_rec_b5, L0_rec_w6, L0_rec_b6, L0_rec_w7, L0_rec_b7, L0_rec_w8, L0_rec_b8, L0_rec_v):
    import jax
    import jax.numpy as jnp

    def _L0_rec_ref(x, label_embedding, w1, b1, w2, w3, b3, w4, w5, b5, w6, b6, w7, b7, w8, b8, v):
        import jax, jax.numpy as jnp
        import numpy as np
        E, U, C, T, N, B, K = (300, 300, 4, 8, 50, 512, 200)
        P = E * (E - 1) // 2
        PAD = jnp.float32(-2 ** 32 + 1)

        def _attn_pool(x, mask, w_a, b_a, w_b):
            score = jnp.exp((x @ w_a + b_a) @ w_b)
            score = jnp.where(mask == 0, PAD, score)
            p = jax.nn.softmax(score, axis=1)
            return jnp.einsum('bne,bn->be', x, p[..., 0])
        mask = jnp.sign(jnp.sum(jnp.abs(x), axis=2))[..., None]
        q1 = _attn_pool(x, mask, w1, b1, w2)
        q2 = _attn_pool(x, mask, w3, b3, w4)
        h = jnp.concatenate([q1, q2], axis=1) @ w5 + b5
        f6 = h @ w6 + b6
        iu, ju = jnp.triu_indices(E, k=1)
        g = (v @ v.T)[iu, ju]
        cross = h[:, iu] * h[:, ju] * g
        f7 = cross @ w7 + b7
        out8 = jnp.concatenate([f6, f7], axis=1) @ w8 + b8
        return jnp.einsum('bu,bku->bk', out8, label_embedding)
    e = jnp.stack([tbl_0[ids[:, 0]], tbl_1[ids[:, 1]], tbl_2[ids[:, 2]], tbl_3[ids[:, 3]], tbl_4[ids[:, 4]], tbl_5[ids[:, 5]], tbl_6[ids[:, 6]], tbl_7[ids[:, 7]], tbl_8[ids[:, 8]], tbl_9[ids[:, 9]], tbl_10[ids[:, 10]], tbl_11[ids[:, 11]], tbl_12[ids[:, 12]], tbl_13[ids[:, 13]], tbl_14[ids[:, 14]], tbl_15[ids[:, 15]], tbl_16[ids[:, 16]], tbl_17[ids[:, 17]], tbl_18[ids[:, 18]], tbl_19[ids[:, 19]], tbl_20[ids[:, 20]], tbl_21[ids[:, 21]], tbl_22[ids[:, 22]], tbl_23[ids[:, 23]], tbl_24[ids[:, 24]], tbl_25[ids[:, 25]], tbl_26[ids[:, 26]], tbl_27[ids[:, 27]], tbl_28[ids[:, 28]], tbl_29[ids[:, 29]], tbl_30[ids[:, 30]], tbl_31[ids[:, 31]], tbl_32[ids[:, 32]], tbl_33[ids[:, 33]], tbl_34[ids[:, 34]], tbl_35[ids[:, 35]], tbl_36[ids[:, 36]], tbl_37[ids[:, 37]], tbl_38[ids[:, 38]], tbl_39[ids[:, 39]], tbl_40[ids[:, 40]], tbl_41[ids[:, 41]], tbl_42[ids[:, 42]], tbl_43[ids[:, 43]], tbl_44[ids[:, 44]], tbl_45[ids[:, 45]], tbl_46[ids[:, 46]], tbl_47[ids[:, 47]], tbl_48[ids[:, 48]], tbl_49[ids[:, 49]]], axis=1)
    z = _L0_rec_ref(e, r_label_embedding, L0_rec_w1, L0_rec_b1, L0_rec_w2, L0_rec_w3, L0_rec_b3, L0_rec_w4, L0_rec_w5, L0_rec_b5, L0_rec_w6, L0_rec_b6, L0_rec_w7, L0_rec_b7, L0_rec_w8, L0_rec_b8, L0_rec_v)
    z = z.reshape(z.shape[0], -1)
    h = jnp.concatenate([z, dense_ctx], axis=1)
    h = jnp.maximum(h @ W_top1 + b_top1, 0.0)
    h = jnp.maximum(h @ W_top2 + b_top2, 0.0)
    y = h @ W_top3
    return y

_drawn_inputs = setup_inputs


def setup_inputs(seed=0):
    import zlib

    import numpy as np

    out = dict(_drawn_inputs(seed))
    spreads = {'b_top1': (0.0, 0.547),
     'b_top2': (0.0, 0.1),
     'L0_rec_b1': (0.0, 0.8),
     'L0_rec_b3': (0.0, 0.8),
     'L0_rec_b5': (0.0, 0.1),
     'L0_rec_b6': (0.0, 0.1),
     'L0_rec_b7': (0.0, 0.1),
     'L0_rec_b8': (0.0, 0.1)}
    factors = {'tbl_0': 8.0,
     'tbl_1': 8.0,
     'tbl_2': 8.0,
     'tbl_3': 8.0,
     'tbl_4': 8.0,
     'tbl_5': 8.0,
     'tbl_6': 8.0,
     'tbl_7': 8.0,
     'tbl_8': 8.0,
     'tbl_9': 8.0,
     'tbl_10': 8.0,
     'tbl_11': 8.0,
     'tbl_12': 8.0,
     'tbl_13': 8.0,
     'tbl_14': 8.0,
     'tbl_15': 8.0,
     'tbl_16': 8.0,
     'tbl_17': 8.0,
     'tbl_18': 8.0,
     'tbl_19': 8.0,
     'tbl_20': 8.0,
     'tbl_21': 8.0,
     'tbl_22': 8.0,
     'tbl_23': 8.0,
     'tbl_24': 8.0,
     'tbl_25': 8.0,
     'tbl_26': 8.0,
     'tbl_27': 8.0,
     'tbl_28': 8.0,
     'tbl_29': 8.0,
     'tbl_30': 8.0,
     'tbl_31': 8.0,
     'tbl_32': 8.0,
     'tbl_33': 8.0,
     'tbl_34': 8.0,
     'tbl_35': 8.0,
     'tbl_36': 8.0,
     'tbl_37': 8.0,
     'tbl_38': 8.0,
     'tbl_39': 8.0,
     'tbl_40': 8.0,
     'tbl_41': 8.0,
     'tbl_42': 8.0,
     'tbl_43': 8.0,
     'tbl_44': 8.0,
     'tbl_45': 8.0,
     'tbl_46': 8.0,
     'tbl_47': 8.0,
     'tbl_48': 8.0,
     'tbl_49': 8.0,
     'L0_rec_w1': 8.0,
     'L0_rec_w2': 8.0,
     'L0_rec_w3': 8.0,
     'L0_rec_w4': 8.0,
     'L0_rec_w5': 5.232}
    for name, (base, spread) in spreads.items():
        noise = np.random.default_rng([zlib.crc32(name.encode()), seed]).standard_normal(out[name].shape)
        drawn = base * np.exp(spread * noise) if base else spread * noise
        out[name] = jnp.asarray(drawn.astype(out[name].dtype))
    for name, factor in factors.items():
        out[name] = (out[name] * factor).astype(out[name].dtype)
    return out
```

```python
from contextlib import ExitStack

import numpy as np

import concourse.bass as bass
from concourse import mybir

F32 = mybir.dt.float32
I32 = mybir.dt.int32
ALU = mybir.AluOpType
ACT = mybir.ActivationFunctionType
AX = mybir.AxisListType

P = 128
B, F, E, K = 512, 50, 300, 200
T = 8
C = 4
BT = B // P
EC, ECH = 3, E // 3
CTX, H1, H2 = 16, 512, 256
KZ = K // 2
PAD = float(np.float32(-2 ** 32 + 1))

PAIRS = E * (E - 1) // 2
DG, TP = 5, 125
TR = DG * E // TP
ROUNDS = -(-PAIRS // (DG * E))
LAST = PAIRS - (ROUNDS - 1) * DG * E
TLAST = -(-LAST // TP)
PLAST = LAST - (TLAST - 1) * TP
HW = E + E // 2

GF = 10
FG = F // GF
DR = 10
JR, AJR = 4, 2
XB = 3
CR = 4
LK = 10
LR = 10
LC = K // LK
assert TR % XB == 0 and TR % CR == 0 and LC == 2 * LR and LR * LK * E == 2 * F * E


def pair_order():
    q = np.arange(ROUNDS * DG * E)
    i, d = q % E, q // E + 1
    return i, (i + d) % E, q < PAIRS


def build(nc, a, out):
    with ExitStack() as ctx:
        def sb(name, shape, dt=F32):
            return ctx.enter_context(nc.sbuf_tensor(name, shape, dt))

        def pb(name, shape):
            return ctx.enter_context(nc.psum_tensor(name, shape, F32))

        def sem(name):
            return ctx.enter_context(nc.semaphore(name))

        stream = sb("stream", [P, 2, F * E])
        x = stream
        lab = stream[:, :, :].rearrange("p s (r n) -> p (s r) n", r=LR // 2)
        w7 = sb("w7", [P, 2, TR * E])
        junk = w7[:, 1, 0:JR * E].rearrange("p (r e) -> p r e", r=JR)
        ajunk = w7[:, 1, 4 * E:(4 + AJR) * E].rearrange("p (r e) -> p r e", r=AJR)
        q_sb = w7[:, 1, 6 * E:8 * E].rearrange("p (a e) -> p a e", a=2)
        qT = w7[0:ECH, 1, 8 * E:8 * E + 2 * EC * P].rearrange("p (c b) -> p c b", c=2 * EC)
        cross = sb("cross", [P, BT, DG * E])
        flat = cross[:, :, :].rearrange("p t n -> p (t n)")
        diag = flat[:, 0:DR * 2 * P].rearrange("p (r a n) -> p r a n", r=DR, a=2)
        o = DR * 2 * P
        wsc = flat[:, o:o + 2 * (E + 1)].rearrange("p (a n) -> p a n", a=2)
        vi, vj = (stream[:, 1, n * ROUNDS * TR * C:(n + 1) * ROUNDS * TR * C]
                  .rearrange("p (n c) -> p n c", c=C) for n in range(2))
        wt1 = flat[0:KZ, 0:2 * H1].rearrange("p (c n) -> p c n", c=2)
        wt1c = flat[0:CTX, 2 * H1:3 * H1]
        ctxT = flat[0:CTX, 3 * H1:3 * H1 + B]
        wt2 = flat[:, 4 * H1:4 * H1 + 4 * H2].rearrange("p (c n) -> p c n", c=4)
        wt3 = flat[:, 4 * H1 + 4 * H2:4 * H1 + 4 * H2 + 2]
        bt1 = flat[:, 4 * H1 + 4 * H2 + 2:4 * H1 + 4 * H2 + 6]
        bt2 = flat[:, 4 * H1 + 4 * H2 + 6:4 * H1 + 4 * H2 + 8]
        crossT = sb("crossT", [P, CR, B])
        w5 = crossT[0:ECH, :, :].rearrange("p r b -> p (r b)")[:, 0:2 * EC * E].rearrange("p (c e) -> p c e", c=2 * EC)
        w6 = sb("w6", [ECH, EC, E])
        w8 = sb("w8", [ECH, 2 * EC, E])
        hh = sb("hh", [P, BT, HW])
        g = sb("g", [P, ROUNDS * TR])
        ident = sb("ident", [P, P])
        brow = sb("brow", [1, 4, E])
        ones = sb("ones", [1, P])
        z = sb("z", [P, K])
        o8 = sb("o8", [P, E])
        ids = sb("ids", [P, BT, F], I32)
        sa = sb("sa", [P, 2, F])
        es = sb("es", [P, 2, F])
        pr = sb("pr", [P, 2, 2, F])
        absum = sb("absum", [P, F])
        padded = sb("padded", [P, F], I32)
        padrow = sb("padrow", [P, F])
        nmax = sb("nmax", [P, 2])
        psum_ = sb("psum_", [P, 2])
        rden = sb("rden", [P, 2, 2])
        wf = w7[:, 0, :]
        hcur, f7s, f6s = wf[:, 0:E], wf[:, E:2 * E], wf[:, 2 * E:3 * E]
        hT, f7T, f6T = (wf[0:ECH, 3 * E + n * EC * P:3 * E + (n + 1) * EC * P]
                        .rearrange("p (c b) -> p c b", c=EC) for n in range(3))
        wg = w7[:, 1, :]
        zT = wg[0:KZ, 0:2 * P].rearrange("p (c b) -> p c b", c=2)
        h1T = wg[:, 2 * P:6 * P].rearrange("p (c b) -> p c b", c=4)
        h2T = wg[:, 6 * P:8 * P].rearrange("p (c b) -> p c b", c=2)
        y_sb = wg[0:1, 8 * P:8 * P + B]
        w12 = w7[0:T, 1, 6 * E:6 * E + 2 * P].rearrange("p (a n) -> p a n", a=2)
        wsw = w7[0:T, 1, 6 * E + 2 * P:6 * E + 2 * P + 2 * (E + 1)].rearrange("p (a n) -> p a n", a=2)

        acc = pb("acc", [P, BT, 512])
        xp = pb("xp", [P, XB, 512])
        po8 = pb("po8", [P, 512])

        s_ids = sem("ids_loaded")
        s_pre = sem("pool_weights_loaded")
        s_v = sem("v_loaded")
        s_wa = sem("w5_w6_w8_loaded")
        s_top = sem("top_weights_loaded")
        s_gat = [[sem(f"gathered_{s}_{n}") for n in range(FG)] for s in range(2)]
        s_w7 = [sem(f"w7_loaded_{s}") for s in range(2)]
        s_lab = [sem(f"labels_loaded_{s}") for s in range(LR)]
        s_ident = sem("ident_ready")
        s_wsp = sem("score_weights_summed")
        s_wsc = sem("score_weights_ready")
        s_g = sem("g_ready")
        s_gp = sem("g_product_ready")
        s_jf = sem("junk_free")
        s_ajf = sem("act_junk_free")
        s_df = sem("diag_free")
        s_sc = sem("scores_ready")
        s_e1 = sem("score_exp_ready")
        s_ab = sem("abs_ready")
        s_ms = sem("mask_steps")
        s_mx = sem("max_ready")
        s_p = sem("softmax_exp_ready")
        s_rd = sem("rden_ready")
        s_d = [sem("diag1_ready"), sem("diag2_ready")]
        s_pool = sem("pools_summed")
        s_qe = sem("q_evacuated")
        s_qt = sem("q_transposed")
        s_qte = sem("qT_evacuated")
        s_h = sem("h_summed")
        s_he = sem("h_evacuated")
        s_cr = sem("cross_ready")
        s_xt = sem("cross_transposed")
        s_ce = sem("crossT_ready")
        s_cf = sem("crossT_free")
        s_ch = sem("chain_products")
        s_che = sem("chain_evacuated")
        s_o8 = sem("o8_summed")
        s_o8t = sem("o8_taken")
        s_lu = sem("labels_used")
        s_z = sem("z_ready")
        s_zt = sem("z_taken")
        s_ml = sem("tower_products")
        s_mle = sem("tower_evacuated")
        s_out = sem("out_written")

        block = ctx.enter_context(nc.Block())

        def scored(t):
            return 2 * F * t

        @block.sync
        def _(sp):
            sp.dma_start(ids[:, :, :], a["ids"].rearrange("(t p) f -> p t f", p=P)).then_inc(s_ids, 16)
            sp.dma_start(w12[:, :, :], a["w24"]).then_inc(s_pre, 16)
            sp.dma_start(wsw[:, :, :], a["w13"]).then_inc(s_pre, 16)
            sp.dma_start(vi, a["vi"]).then_inc(s_v, 16)
            sp.dma_start(vj, a["vj"]).then_inc(s_v, 16)
            sp.dma_start(w5, a["w5"].rearrange("(c p) e -> p c e", p=ECH)).then_inc(s_wa, 16)
            sp.dma_start(w6[:, :, :], a["w6"].rearrange("(c p) e -> p c e", p=ECH)).then_inc(s_wa, 16)
            sp.dma_start(w8[:, :, :], a["w8"].rearrange("(c p) e -> p c e", p=ECH)).then_inc(s_wa, 16)
            for n, name in enumerate(("b5", "b6", "b7", "b8")):
                sp.dma_start(brow[0:1, n, :], a[name].rearrange("(o e) -> o e", o=1)).then_inc(s_wa, 16)
            sp.dma_start(w7[:, 0, :], a["w7"][0]).then_inc(s_w7[0], 16)
            sp.wait_ge(s_he, BT)
            sp.dma_start(w7[:, 1, :], a["w7"][1]).then_inc(s_w7[1], 16)
            lab_d = a["lab"].rearrange("(t p) (h s n) -> t h s p n", p=P, h=2, s=LR)
            for s in range(LR):
                sp.dma_start(lab[:, s, :], lab_d[0, 0, s]).then_inc(s_lab[s], 16)
            with sp.Fori(1, ROUNDS // 2) as r:
                for s in range(2):
                    sp.wait_ge(s_cf, TR * (2 * r + s - 1) + CR)
                    sp.dma_start(w7[:, s, :], a["w7"][bass.ds(2 * r + s, 1), :, :].rearrange("r p n -> (r p) n"))\
                      .then_inc(s_w7[s], 16)
            sp.wait_ge(s_xt, TR * (ROUNDS - 1) + TLAST)
            sp.dma_start(wt1, a["wt1"][0:K, :].rearrange("(c p) n -> p c n", p=KZ)).then_inc(s_top, 16)
            sp.dma_start(wt1c, a["wt1"][K:K + CTX, :]).then_inc(s_top, 16)
            sp.dma_start(ctxT, a["ctxT"]).then_inc(s_top, 16)
            sp.dma_start(wt2, a["wt2"].rearrange("(c p) n -> p c n", p=P)).then_inc(s_top, 16)
            sp.dma_start(wt3, a["wt3"]).then_inc(s_top, 16)
            sp.dma_start(bt1, a["bt1"]).then_inc(s_top, 16)
            sp.dma_start(bt2, a["bt2"]).then_inc(s_top, 16)

            def load_labels(t, half):
                for s in range(LR):
                    sp.wait_ge(s_lu, LR * (2 * t + half - 1) + s + 1)
                    src = lab_d[t, half, s] if isinstance(t, int) else \
                        lab_d[bass.ds(t, 1), half, s].rearrange("t p n -> (t p) n")
                    sp.dma_start(lab[:, s, :], src).then_inc(s_lab[s], 16)

            with sp.Fori(0, BT - 1) as t:
                load_labels(t, 1)
                load_labels(t + 1, 0)
            load_labels(BT - 1, 1)
            sp.wait_ge(s_mle, 4 * BT)
            sp.dma_start(out.rearrange("b o -> o b"), y_sb).then_inc(s_out, 16)
            sp.wait_ge(s_out, 16)

        @block.gpsimd
        def _(pool):
            pool.memset(ident[:, :], 0.0).then_inc(s_ident, 1)
            pool.memset(ones[:, :], 1.0).then_inc(s_ident, 1)
            pool.wait_ge(s_ident, 2)
            pool.affine_select(out=ident[:, :], in_=ident[:, :], compare_op=ALU.not_equal, fill=1.0, base=0,
                               pattern=[[-1, P]], channel_multiplier=1).then_inc(s_ident, 1)
            pool.wait_ge(s_ids, 16)
            for t in range(BT):
                if t == 1:
                    pool.wait_ge(s_g, 1)
                for f in range(F):
                    if t >= 2 and f % GF == 0:
                        pool.wait_ge(s_df, F * (t - 2) + f + GF + DR)
                    pool.indirect_dma_start(x[:, t % 2, f * E:(f + 1) * E], None, a[f"tbl_{f}"],
                                            bass.IndirectOffsetOnAxis(ids[:, t, f:f + 1], 0))\
                        .then_inc(s_gat[t % 2][f // GF], 16)

        @block.vector
        def _(dve):
            dve.memset(padrow[:, :], PAD).then_inc(s_jf, JR)
            dve.wait_ge(s_v, 32)
            dve.tensor_tensor(vi, vi, vj, ALU.mult).then_inc(s_gp, 1)
            dve.wait_ge(s_gp, 1)
            dve.tensor_reduce(g[:, :], vi, AX.X, ALU.add).then_inc(s_g, 1)
            dve.wait_ge(s_wsp, 1)
            for n in range(2):
                dve.tensor_copy(wsc[:, n, :], acc[:, n, 0:E + 1]).then_inc(s_wsc, 1)
            dve.wait_ge(s_wsc, 2)

            def score(t, n, j):
                for s in range(2):
                    m = 2 * j + s
                    dve.wait_ge(s_jf, scored(t) + 2 * (n - j) + m + 1)
                    dve.scalar_tensor_tensor(junk[:, m % JR, :], x[:, t % 2, bass.ds(n * E, E)], 1.0,
                                             wsc[:, s, 0:E], ALU.mult, ALU.mult,
                                             accum_out=sa[:, s, bass.ds(n, 1)]).then_inc(s_jf, 1)

            def gathered(t):
                for grp in range(FG):
                    dve.wait_ge(s_gat[t % 2][grp], 16 * GF * (t // 2 + 1))

            def softmax(t):
                dve.wait_ge(s_jf, scored(t + 1) + JR)
                dve.wait_ge(s_ab, t + 1)
                dve.tensor_scalar(padded[:, :], absum[:, :], 0.0, None, ALU.is_equal).then_inc(s_ms, 1)
                dve.wait_ge(s_ms, 4 * t + 1)
                dve.wait_ge(s_e1, 2 * (t + 1))
                for s in range(2):
                    dve.copy_predicated(es[:, s, :], padded[:, :], padrow[:, :]).then_inc(s_ms, 1)
                dve.wait_ge(s_ms, 4 * t + 3)
                dve.tensor_reduce(nmax[:, :], es[:, :, :], AX.X, ALU.max).then_inc(s_ms, 1)
                dve.wait_ge(s_ms, 4 * t + 4)
                dve.tensor_scalar(nmax[:, :], nmax[:, :], -1.0, None, ALU.mult).then_inc(s_mx, 1)
                dve.wait_ge(s_p, 2 * (t + 1))
                dve.reciprocal(rden[:, t % 2, :], psum_[:, :]).then_inc(s_rd, 1)

            gathered(0)
            with dve.Fori(0, FG) as grp:
                for j in range(GF):
                    score(0, GF * grp + j, j)
            softmax(0)
            dve.wait_ge(s_ident, 3)
            for t in range(BT):
                if t + 1 < BT:
                    gathered(t + 1)
                    dve.wait_ge(s_e1, 2 * (t + 1))
                with dve.Fori(0, FG) as grp:
                    for j in range(GF):
                        n = GF * grp + j
                        dve.wait_ge(s_df, F * t + n + 1)
                        dve.tensor_scalar(diag[:, j, 0, :], ident[:, :], pr[:, t % 2, 0, bass.ds(n, 1)], None,
                                          ALU.mult).then_inc(s_d[0], 1)
                        if t + 1 < BT:
                            score(t + 1, n, j)
                if t + 1 < BT:
                    softmax(t + 1)

            dve.wait_ge(s_he, BT)

            def products(r, after):
                for d in range(DG):
                    if after:
                        last = min((E * (d + 1) - 1) // TP, TR - 1)
                        dve.wait_ge(s_xt, TR * (r - 1) + last + 1)
                    dve.tensor_tensor(cross[:, :, d * E:(d + 1) * E], hh[:, :, 0:E],
                                      hh[:, :, bass.ds(DG * r + d + 1, E)], ALU.mult).then_inc(s_cr, 1)

            products(0, False)
            with dve.Fori(1, ROUNDS) as r:
                products(r, True)

            with dve.Fori(0, BT) as t:
                dve.wait_ge(s_o8, t + 1)
                dve.wait_ge(s_zt, t + 1)
                dve.tensor_copy(o8[:, :], po8[:, 0:E]).then_inc(s_o8t, 1)
                dve.wait_ge(s_o8t, t + 1)
                for c in range(LC):
                    dve.wait_ge(s_lab[c % LR], 16 * (2 * t + c // LR + 1))
                    for k in range(LK):
                        sl = lab[:, c % LR, k * E:(k + 1) * E]
                        col = c * LK + k
                        ins = dve.tensor_tensor_reduce(sl, sl, o8[:, :], 1.0, 0.0, ALU.mult, ALU.add,
                                                       z[:, col:col + 1])
                    ins.then_inc(s_lu, 1)
                dve.wait_ge(s_lu, LC * (t + 1))
                dve.nop().then_inc(s_z, 1)

        @block.scalar
        def _(act):
            act.wait_ge(s_wsc, 2)

            def absum_of(t, n, j):
                act.wait_ge(s_ajf, F * t + n + 1)
                act.activation(ajunk[:, j % AJR, :], x[:, t % 2, bass.ds(n * E, E)], ACT.Abs,
                               accum_out=absum[:, bass.ds(n, 1)]).then_inc(s_ajf, 1)

            def gathered(t):
                for grp in range(FG):
                    act.wait_ge(s_gat[t % 2][grp], 16 * GF * (t // 2 + 1))

            def softmax(t):
                act.wait_ge(s_ajf, F * (t + 1) + AJR)
                act.nop().then_inc(s_ab, 1)
                act.wait_ge(s_jf, scored(t + 1) + JR)
                for s in range(2):
                    act.activation(es[:, s, :], sa[:, s, :], ACT.Exp, bias=wsc[:, s, E:E + 1]).then_inc(s_e1, 1)
                act.wait_ge(s_mx, t + 1)
                for s in range(2):
                    act.activation(pr[:, t % 2, s, :], es[:, s, :], ACT.Exp, bias=nmax[:, s:s + 1],
                                   accum_out=psum_[:, s:s + 1]).then_inc(s_p, 1)

            def tail(t):
                act.wait_ge(s_pool, t + 1)
                act.wait_ge(s_rd, t + 1)
                for s in range(2):
                    act.activation(q_sb[:, s, :], acc[:, 2 * (t % 2) + s, 0:E], ACT.Copy,
                                   scale=rden[:, t % 2, s:s + 1]).then_inc(s_qe, 1)
                act.wait_ge(s_qt, t + 1)
                for s in range(2):
                    act.activation(qT[:, EC * s:EC * (s + 1), :],
                                   xp[0:ECH, s, 0:EC * P].rearrange("p (c b) -> p c b", c=EC), ACT.Copy)\
                       .then_inc(s_qte, 1)
                act.wait_ge(s_h, t + 1)
                act.activation(hh[:, t, 0:E], xp[:, 2, 0:E], ACT.Copy)
                act.activation(hh[:, t, E:HW], xp[:, 2, 0:HW - E], ACT.Copy).then_inc(s_he, 1)

            gathered(0)
            with act.Fori(0, FG) as grp:
                for j in range(GF):
                    absum_of(0, GF * grp + j, j)
            softmax(0)
            act.wait_ge(s_ident, 3)
            for t in range(BT):
                act.wait_ge(s_p, 2 * (t + 1))
                if t + 1 < BT:
                    gathered(t + 1)
                    act.wait_ge(s_ms, 4 * (t + 1))
                with act.Fori(0, FG) as grp:
                    for j in range(GF):
                        n = GF * grp + j
                        act.wait_ge(s_df, F * t + n + 1)
                        act.activation(diag[:, j, 1, :], ident[:, :], ACT.Copy,
                                       scale=pr[:, t % 2, 1, bass.ds(n, 1)]).then_inc(s_d[1], 1)
                        if t + 1 < BT:
                            absum_of(t + 1, n, j)
                if t + 1 < BT:
                    softmax(t + 1)
                tail(t)

            act.wait_ge(s_g, 1)

            def evacuate(r, k, rows):
                n = TR * r + k
                act.wait_ge(s_xt, n + 1)
                act.wait_ge(s_cf, n + 1)
                act.activation(crossT[0:rows, k % CR, :], xp[0:rows, k % XB, :], ACT.Copy,
                               scale=g[0:rows, bass.ds(n, 1)]).then_inc(s_ce, 1)

            with act.Fori(0, ROUNDS - 1) as r:
                for k in range(TR):
                    evacuate(r, k, TP)
            for k in range(TLAST):
                evacuate(ROUNDS - 1, k, TP if k + 1 < TLAST else PLAST)

            def chain(t):
                act.wait_ge(s_cf, TR * (ROUNDS - 1) + TLAST + CR)
                act.activation(hcur, hh[:, bass.ds(t, 1), 0:E].rearrange("p t e -> p (t e)"), ACT.Copy)
                act.activation(f7s, acc[:, bass.ds(t, 1), 0:E].rearrange("p t e -> p (t e)"), ACT.Copy).then_inc(s_che, 1)
                act.wait_ge(s_ch, 3 * t + 1)
                act.activation(hT, xp[0:ECH, 0, 0:EC * P].rearrange("p (c b) -> p c b", c=EC), ACT.Copy)
                act.activation(f7T, xp[0:ECH, 1, 0:EC * P].rearrange("p (c b) -> p c b", c=EC), ACT.Copy)\
                   .then_inc(s_che, 1)
                act.wait_ge(s_ch, 3 * t + 2)
                act.activation(f6s, xp[:, 2, 0:E], ACT.Copy).then_inc(s_che, 1)
                act.wait_ge(s_ch, 3 * t + 3)
                act.activation(f6T, xp[0:ECH, 0, 0:EC * P].rearrange("p (c b) -> p c b", c=EC), ACT.Copy)\
                   .then_inc(s_che, 1)

            def tower(t):
                act.wait_ge(s_ml, 4 * t + 1)
                act.activation(zT, xp[0:KZ, 0, 0:2 * P].rearrange("p (c b) -> p c b", c=2), ACT.Copy)\
                   .then_inc(s_mle, 1)
                act.wait_ge(s_top, 16 * 7)
                act.wait_ge(s_ml, 4 * t + 2)
                for m in range(4):
                    ins = act.activation(h1T[:, m, :], xp[:, 1, m * P:(m + 1) * P], ACT.Relu, bias=bt1[:, m:m + 1])
                ins.then_inc(s_mle, 1)
                act.wait_ge(s_ml, 4 * t + 3)
                for m in range(2):
                    ins = act.activation(h2T[:, m, :], xp[:, 2, m * P:(m + 1) * P], ACT.Relu, bias=bt2[:, m:m + 1])
                ins.then_inc(s_mle, 1)
                act.wait_ge(s_ml, 4 * t + 4)
                act.activation(y_sb[:, bass.ds(t * P, P)], xp[0:1, 0, 0:P], ACT.Copy).then_inc(s_mle, 1)

            chain(0)
            with act.Fori(0, BT - 1) as t:
                act.wait_ge(s_o8, t + 1)
                chain(t + 1)
                tower(t)
            tower(BT - 1)

        @block.tensor
        def _(pe):
            pe.wait_ge(s_pre, 32)
            for n in range(2):
                ins = pe.matmul(acc[:, n, 0:E + 1], w12[:, n, :], wsw[:, n, :], start=True, stop=True)
            ins.then_inc(s_wsp, 1)
            pe.wait_ge(s_ident, 3)
            pe.wait_ge(s_wa, 16 * 7)
            pe.wait_ge(s_wsc, 2)
            pe.nop().then_inc(s_df, DR)
            pe.nop().then_inc(s_cf, CR)
            pe.nop().then_inc(s_ajf, AJR)
            pe.nop().then_inc(s_zt, 1)
            for t in range(BT):
                gat = s_gat[t % 2]
                for grp in range(FG):
                    pe.wait_ge(gat[grp], 16 * GF * (t // 2 + 1))

                def weighted(f, j, start, stop):
                    for s in range(2):
                        pe.wait_ge(s_d[s], F * t + f + 1)
                        ins = pe.matmul(acc[:, 2 * (t % 2) + s, 0:E], diag[:, j, s, :],
                                        x[:, t % 2, bass.ds(f * E, E)], start=start, stop=stop,
                                        skip_group_check=True)
                    ins.then_inc(s_df, 1)

                for j in range(GF):
                    weighted(j, j, j == 0, False)
                with pe.Fori(1, FG) as grp:
                    for j in range(GF):
                        weighted(GF * grp + j, j, False, j == GF - 1)
                pe.wait_ge(s_df, F * (t + 1) + DR)
                pe.nop().then_inc(s_pool, 1)
                pe.wait_ge(s_qe, 2 * (t + 1))
                for s in range(2):
                    for c in range(EC):
                        ins = pe.transpose(xp[0:ECH, s, c * P:(c + 1) * P], q_sb[:, s, c * ECH:(c + 1) * ECH], ident[:, :])
                ins.then_inc(s_qt, 1)
                pe.wait_ge(s_qte, 2 * (t + 1))
                pe.matmul(xp[:, 2, 0:E], ones[:, :], brow[:, 0, :], start=True, stop=False)
                for c in range(2 * EC):
                    ins = pe.matmul(xp[:, 2, 0:E], qT[:, c, :], w5[:, c, :], start=False, stop=c == 2 * EC - 1)
                ins.then_inc(s_h, 1)
            pe.wait_ge(s_he, BT)

            for t in range(BT):
                pe.matmul(acc[:, t, 0:E], ones[:, :], brow[:, 2, :], start=True, stop=False, skip_group_check=True)

            def transpose(r, k, rows):
                lo, hi = TP * k // E, (TP * k + rows - 1) // E
                if k == 0 or hi > (TP * k - 1) // E:
                    pe.wait_ge(s_cr, DG * r + hi + 1)
                for t in range(BT):
                    ins = pe.transpose(xp[0:rows, k % XB, t * P:(t + 1) * P], cross[:, t, TP * k:TP * k + rows], ident[:, :])
                ins.then_inc(s_xt, 1)

            def multiply(r, k, rows, slot, last=False):
                pe.wait_ge(s_ce, TR * r + k + 1)
                for t in range(BT):
                    ins = pe.matmul(acc[:, t, 0:E], crossT[0:rows, k % CR, t * P:(t + 1) * P],
                                    w7[0:rows, slot, k * E:(k + 1) * E], start=False, stop=last, skip_group_check=True)
                ins.then_inc(s_cf, 1)

            def round_(r, slot):
                pe.wait_ge(s_w7[slot], 16 * ((r - slot) // 2 + 1) if isinstance(r, int) else 16 * (r2 + 1))
                for k in range(TR):
                    if k + 2 < TR:
                        transpose(r, k + 2, TP)
                    elif not isinstance(r, int) or r + 1 < ROUNDS:
                        transpose(r + 1, k + 2 - TR, TP)
                    multiply(r, k, TP, slot)

            transpose(0, 0, TP)
            transpose(0, 1, TP)
            with pe.Fori(0, ROUNDS // 2 - 1) as r2:
                round_(2 * r2, 0)
                round_(2 * r2 + 1, 1)
            round_(ROUNDS - 2, 0)
            pe.wait_ge(s_w7[1], 16 * (ROUNDS // 2))
            for k in range(TLAST):
                if k + 2 < TLAST:
                    transpose(ROUNDS - 1, k + 2, TP if k + 3 < TLAST else PLAST)
                multiply(ROUNDS - 1, k, TP if k + 1 < TLAST else PLAST, 1, last=k + 1 == TLAST)

            def chain(t):
                pe.wait_ge(s_che, 4 * t + 1)
                for s, src in enumerate((hcur, f7s)):
                    for c in range(EC):
                        ins = pe.transpose(xp[0:ECH, s, c * P:(c + 1) * P], src[:, c * ECH:(c + 1) * ECH], ident[:, :])
                ins.then_inc(s_ch, 1)
                pe.wait_ge(s_che, 4 * t + 2)
                pe.matmul(xp[:, 2, 0:E], ones[:, :], brow[:, 1, :], start=True, stop=False)
                for c in range(EC):
                    ins = pe.matmul(xp[:, 2, 0:E], hT[:, c, :], w6[:, c, :], start=False, stop=c == EC - 1)
                ins.then_inc(s_ch, 1)
                pe.wait_ge(s_che, 4 * t + 3)
                for c in range(EC):
                    ins = pe.transpose(xp[0:ECH, 0, c * P:(c + 1) * P], f6s[:, c * ECH:(c + 1) * ECH], ident[:, :])
                ins.then_inc(s_ch, 1)
                pe.wait_ge(s_che, 4 * t + 4)
                if not isinstance(t, int):
                    pe.wait_ge(s_o8t, t)
                pe.matmul(po8[:, 0:E], ones[:, :], brow[:, 3, :], start=True, stop=False)
                for c in range(2 * EC):
                    left = f6T[:, c, :] if c < EC else f7T[:, c - EC, :]
                    ins = pe.matmul(po8[:, 0:E], left, w8[:, c, :], start=False, stop=c == 2 * EC - 1)
                ins.then_inc(s_o8, 1)

            def tower(t):
                pe.wait_ge(s_z, t + 1)
                for c in range(2):
                    ins = pe.transpose(xp[0:KZ, 0, c * P:(c + 1) * P], z[:, c * KZ:(c + 1) * KZ], ident[:, :])
                ins.then_inc(s_ml, 1)
                pe.wait_ge(s_ml, 4 * t + 1)
                pe.nop().then_inc(s_zt, 1)
                pe.wait_ge(s_mle, 4 * t + 1)
                pe.wait_ge(s_top, 16 * 7)
                for m in range(4):
                    ms = slice(m * P, (m + 1) * P)
                    for c in range(2):
                        pe.matmul(xp[:, 1, ms], wt1[:, c, ms], zT[:, c, :], start=c == 0, stop=False)
                    ins = pe.matmul(xp[:, 1, ms], wt1c[:, ms], ctxT[:, bass.ds(t * P, P)], start=False, stop=True)
                ins.then_inc(s_ml, 1)
                pe.wait_ge(s_mle, 4 * t + 2)
                for m in range(2):
                    for c in range(4):
                        ins = pe.matmul(xp[:, 2, m * P:(m + 1) * P], wt2[:, c, m * P:(m + 1) * P], h1T[:, c, :],
                                        start=c == 0, stop=c == 3)
                ins.then_inc(s_ml, 1)
                pe.wait_ge(s_mle, 4 * t + 3)
                for c in range(2):
                    ins = pe.matmul(xp[0:1, 0, 0:P], wt3[:, c:c + 1], h2T[:, c, :], start=c == 0, stop=c == 1)
                ins.then_inc(s_ml, 1)
                pe.wait_ge(s_mle, 4 * t + 4)

            chain(0)
            with pe.Fori(0, BT - 1) as t:
                chain(t + 1)
                tower(t)
            tower(BT - 1)


def layout(inputs):
    f = {k: np.ascontiguousarray(v) for k, v in inputs.items()}
    i, j, there = pair_order()
    lo, hi = np.minimum(i, j), np.maximum(i, j)
    row = np.where(there, lo * (2 * E - 1 - lo) // 2 + hi - lo - 1, PAIRS)
    grid = np.full((ROUNDS, TR, P), PAIRS)
    grid[:, :, 0:TP] = row.reshape(ROUNDS, TR, TP)
    w7 = np.concatenate([f["L0_rec_w7"], np.zeros((1, E), np.float32)])
    d = {f"tbl_{n}": f[f"tbl_{n}"] for n in range(F)}
    d["w7"] = w7[grid.transpose(0, 2, 1)].reshape(ROUNDS, P, TR * E)
    v = np.concatenate([f["L0_rec_v"], np.zeros((1, C), np.float32)])
    for name, n in (("vi", i), ("vj", j)):
        at = np.full((ROUNDS, TR, P), E)
        at[:, :, 0:TP] = np.where(there, n, E).reshape(ROUNDS, TR, TP)
        d[name] = np.ascontiguousarray(v[at.reshape(ROUNDS * TR, P).T])
    d["ids"] = f["ids"]
    d["w13"] = np.stack([np.concatenate([f[f"L0_rec_w{n}"].T, f[f"L0_rec_b{n}"][:, None]], 1) for n in (1, 3)], 1)
    d["w24"] = np.stack([np.repeat(f[f"L0_rec_w{n}"], P, 1) for n in (2, 4)], 1)
    for n in (5, 6, 8):
        d[f"w{n}"] = f[f"L0_rec_w{n}"]
    for n in (5, 6, 7, 8):
        d[f"b{n}"] = f[f"L0_rec_b{n}"]
    d["lab"] = f["r_label_embedding"].reshape(B, K * E)
    d["wt1"], d["wt2"] = f["W_top1"], f["W_top2"]
    d["wt3"] = np.ascontiguousarray(f["W_top3"].reshape(2, P).T)
    d["bt1"] = np.ascontiguousarray(f["b_top1"].reshape(4, P).T)
    d["bt2"] = np.ascontiguousarray(f["b_top2"].reshape(2, P).T)
    d["ctxT"] = np.ascontiguousarray(f["dense_ctx"].T)
    return {k: np.ascontiguousarray(x) for k, x in d.items()}


def kernel(**inputs):
    import concourse.bacc as bacc
    from concourse.bass_utils import run_bass_kernel_spmd

    nc = bacc.Bacc("TRN2", target_bir_lowering=False, num_devices=1)
    arrays = layout({k: np.asarray(v) for k, v in inputs.items()})
    aps = {k: nc.dram_tensor(f"in_{k}", v.shape, mybir.dt.from_np(v.dtype), kind="ExternalInput").ap()
           for k, v in arrays.items()}
    out = nc.dram_tensor("out_y", (B, 1), F32, kind="ExternalOutput").ap()
    build(nc, aps, out)
    r = run_bass_kernel_spmd(nc, [{f"in_{k}": v for k, v in arrays.items()}], core_ids=[0])
    return r.results[0]["out_y"]
```

```python
from contextlib import ExitStack

import numpy as np

import concourse.bass as bass
from concourse import mybir

F32 = mybir.dt.float32
F32R = mybir.dt.float32r
I32 = mybir.dt.int32
ALU = mybir.AluOpType
ACT = mybir.ActivationFunctionType
AX = mybir.AxisListType

P = 128
B, F, E, K = 512, 50, 300, 200
T = 8
C = 4
BT = B // P
EC, ECH = 3, E // 3
CTX, H1, H2 = 16, 512, 256
KZ = K // 2
PAD = float(np.float32(-2 ** 32 + 1))

PAIRS = E * (E - 1) // 2
DG, TP = 5, 125
TR = DG * E // TP
ROUNDS = -(-PAIRS // (DG * E))
LAST = PAIRS - (ROUNDS - 1) * DG * E
TLAST = -(-LAST // TP)
PLAST = LAST - (TLAST - 1) * TP
HW = E + E // 2

TH = TR // 2
GF = 10
FG = F // GF
GR = 8
DR = 5
JR = 2
XB = 3
CR = 3
LK = 10
LR = 8
LC = K // LK
assert TR % XB == 0 and TR % CR == 0 and (2 * LC) % LR == 0 and LK == GF and GF == 2 * DR and DR * 2 % JR == 0


def pair_order():
    q = np.arange(ROUNDS * DG * E)
    i, d = q % E, q // E + 1
    return i, (i + d) % E, q < PAIRS


def build(nc, a, out):
    with ExitStack() as ctx:
        def sb(name, shape, dt=F32):
            return ctx.enter_context(nc.sbuf_tensor(name, shape, dt))

        def pb(name, shape):
            return ctx.enter_context(nc.psum_tensor(name, shape, F32))

        def sem(name):
            return ctx.enter_context(nc.semaphore(name))

        stream = sb("stream", [P, GR, GF * E])
        vi, vj = (stream[:, FG, n * ROUNDS * TR * C:(n + 1) * ROUNDS * TR * C]
                  .rearrange("p (n c) -> p n c", c=C) for n in range(2))
        raw = sb("raw", [P, 2, TH * E])
        w7h = sb("w7h", [P, 2, TH * E], F32R)
        w7l = sb("w7l", [P, 2, TH * E], F32R)
        q_sb = raw[:, 1, 0:2 * E].rearrange("p (a e) -> p a e", a=2)
        f6s = q_sb[:, 0, :]
        qT = raw[0:ECH, 1, 2 * E:2 * E + 2 * EC * P].rearrange("p (c b) -> p c b", c=2 * EC)
        hT, f6T = qT[:, 0:EC, :], qT[:, EC:2 * EC, :]
        w12 = raw[0:T, 1, 0:2 * P].rearrange("p (a n) -> p a n", a=2)
        wsw = raw[0:T, 1, 2 * P:2 * P + 2 * (E + 1)].rearrange("p (a n) -> p a n", a=2)
        cross = sb("cross", [P, BT, DG * E])
        flat = cross[:, :, :].rearrange("p t n -> p (t n)")
        taken = [0]

        def part(n):
            taken[0] += n
            assert taken[0] <= BT * DG * E
            return slice(taken[0] - n, taken[0])

        diag = flat[:, part(DR * 2 * P)].rearrange("p (r a n) -> p r a n", r=DR, a=2)
        wsc = flat[:, part(2 * (E + 1))].rearrange("p (a n) -> p a n", a=2)
        junk = flat[:, part(JR * E)].rearrange("p (r e) -> p r e", r=JR)
        w5 = flat[0:ECH, part(2 * EC * E)].rearrange("p (c e) -> p c e", c=2 * EC)
        w6 = flat[0:ECH, part(EC * E)].rearrange("p (c e) -> p c e", c=EC)
        taken[0] = 0
        wt1 = flat[0:KZ, part(2 * H1)].rearrange("p (c n) -> p c n", c=2)
        wt1c = flat[0:CTX, part(H1)]
        ctxT = flat[0:CTX, part(B)]
        wt2 = flat[:, part(4 * H2)].rearrange("p (c n) -> p c n", c=4)
        wt3, bt1, bt2 = flat[:, part(2)], flat[:, part(4)], flat[:, part(2)]
        f7s = flat[:, part(E)]
        f7T = flat[0:ECH, part(EC * P)].rearrange("p (c b) -> p c b", c=EC)
        zT = flat[0:KZ, part(2 * P)].rearrange("p (c b) -> p c b", c=2)
        h1T = flat[:, part(4 * P)].rearrange("p (c b) -> p c b", c=4)
        h2T = flat[:, part(2 * P)].rearrange("p (c b) -> p c b", c=2)
        y_sb = flat[0:1, part(B)]
        crossTh = sb("crossTh", [P, CR, B], F32R)
        crossTl = sb("crossTl", [P, CR, B], F32R)
        w8 = sb("w8", [ECH, 2 * EC, E])
        hh = sb("hh", [P, BT, HW])
        o6 = sb("o6", [P, BT, E])
        g = sb("g", [P, ROUNDS * TR])
        ident = sb("ident", [P, P])
        brow = sb("brow", [1, 4, E])
        ones = sb("ones", [1, P])
        z = sb("z", [P, K])
        o8 = sb("o8", [P, E])
        ids = sb("ids", [P, BT, F], I32)
        sa = sb("sa", [P, 2, F])
        es = sb("es", [P, 2, F])
        pr = sb("pr", [P, 2, 2, F])
        absum = sb("absum", [P, F])
        padded = sb("padded", [P, F], I32)
        padrow = sb("padrow", [P, F])
        nmax = sb("nmax", [P, 2])
        psum_ = sb("psum_", [P, 2])
        rden = sb("rden", [P, 2, 2])

        acc = pb("acc", [P, BT, 512])
        xp = pb("xp", [P, XB, 512])
        po8 = pb("po8", [P, 512])
        ajunk = po8[:, 0:E]

        s_ids = sem("ids_loaded")
        s_pre = sem("pool_weights_loaded")
        s_v = sem("v_loaded")
        s_wa = sem("w5_w6_w8_loaded")
        s_top = sem("top_weights_loaded")
        s_gat = [sem(f"gathered_{n}") for n in range(GR)]
        s_raw = [sem(f"w7_loaded_{s}") for s in range(2)]
        s_wh = sem("w7_high_ready")
        s_wl = sem("w7_low_ready")
        s_lab = [sem(f"labels_loaded_{s}") for s in range(LR)]
        s_ident = sem("ident_ready")
        s_wsp = sem("score_weights_summed")
        s_wsc = sem("score_weights_ready")
        s_g = sem("g_ready")
        s_gp = sem("g_product_ready")
        s_jf = sem("junk_free")
        s_ajf = sem("act_junk_free")
        s_df = sem("diag_free")
        s_sc = sem("scores_ready")
        s_e1 = sem("score_exp_ready")
        s_ab = sem("abs_ready")
        s_ms = sem("mask_steps")
        s_mx = sem("max_ready")
        s_p = sem("softmax_exp_ready")
        s_rd = sem("rden_ready")
        s_d = [sem("diag1_ready"), sem("diag2_ready")]
        s_pool = sem("pools_summed")
        s_te = sem("tail_evacuated")
        s_tp = sem("tail_products")
        s_cr = sem("cross_ready")
        s_xt = sem("cross_transposed")
        s_ch_ = sem("crossT_high_ready")
        s_cl = sem("crossT_low_ready")
        s_cf = sem("crossT_free")
        s_ch = sem("chain_products")
        s_che = sem("chain_evacuated")
        s_o8 = sem("o8_summed")
        s_o8t = sem("o8_taken")
        s_lu = sem("labels_used")
        s_z = sem("z_ready")
        s_zt = sem("z_taken")
        s_ml = sem("tower_products")
        s_mle = sem("tower_evacuated")
        s_out = sem("out_written")

        block = ctx.enter_context(nc.Block())

        def scored(t):
            return 2 * F * t

        def group(t, n):
            n = FG * t + n
            return n % GR, 16 * GF * (n // GR + 1)

        STEPS = 7
        CHUNKS = BT * LC

        @block.sync
        def _(sp):
            sp.dma_start(ids[:, :, :], a["ids"].rearrange("(t p) f -> p t f", p=P)).then_inc(s_ids, 16)
            sp.dma_start(w12, a["w24"]).then_inc(s_pre, 16)
            sp.dma_start(wsw, a["w13"]).then_inc(s_pre, 16)
            sp.dma_start(vi, a["vi"]).then_inc(s_v, 16)
            sp.dma_start(vj, a["vj"]).then_inc(s_v, 16)
            sp.dma_start(w5, a["w5"].rearrange("(c p) e -> p c e", p=ECH)).then_inc(s_wa, 16)
            sp.dma_start(w6, a["w6"].rearrange("(c p) e -> p c e", p=ECH)).then_inc(s_wa, 16)
            sp.dma_start(w8[:, :, :], a["w8"].rearrange("(c p) e -> p c e", p=ECH)).then_inc(s_wa, 16)
            for n, name in enumerate(("b5", "b6", "b7", "b8")):
                sp.dma_start(brow[0:1, n, :], a[name].rearrange("(o e) -> o e", o=1)).then_inc(s_wa, 16)
            sp.dma_start(raw[:, 0, :], a["w7"][0, 0]).then_inc(s_raw[0], 16)
            sp.wait_ge(s_pool, BT)
            for s in range(LR):
                sp.dma_start(stream[:, s, :], a["lab"][s]).then_inc(s_lab[s], 16)
            sp.wait_ge(s_te, STEPS * BT)
            sp.dma_start(raw[:, 1, :], a["w7"][0, 1]).then_inc(s_raw[1], 16)
            with sp.Fori(1, ROUNDS) as r:
                for s in range(2):
                    sp.wait_ge(s_wl, 2 * r + s - 1)
                    sp.dma_start(raw[:, s, :], a["w7"][bass.ds(r, 1), s, :, :].rearrange("r p n -> (r p) n"))\
                      .then_inc(s_raw[s], 16)
            sp.wait_ge(s_xt, TR * (ROUNDS - 1) + TLAST)
            sp.dma_start(wt1, a["wt1"][0:K, :].rearrange("(c p) n -> p c n", p=KZ)).then_inc(s_top, 16)
            sp.dma_start(wt1c, a["wt1"][K:K + CTX, :]).then_inc(s_top, 16)
            sp.dma_start(ctxT, a["ctxT"]).then_inc(s_top, 16)
            sp.dma_start(wt2, a["wt2"].rearrange("(c p) n -> p c n", p=P)).then_inc(s_top, 16)
            sp.dma_start(wt3, a["wt3"]).then_inc(s_top, 16)
            sp.dma_start(bt1, a["bt1"]).then_inc(s_top, 16)
            sp.dma_start(bt2, a["bt2"]).then_inc(s_top, 16)
            with sp.Fori(1, CHUNKS // LR) as r:
                for s in range(LR):
                    sp.wait_ge(s_lu, LR * (r - 1) + s + 1)
                    sp.dma_start(stream[:, s, :], a["lab"][bass.ds(LR * r + s, 1), :, :].rearrange("c p n -> (c p) n"))\
                      .then_inc(s_lab[s], 16)
            sp.wait_ge(s_mle, 4 * BT)
            sp.dma_start(out.rearrange("b o -> o b"), y_sb).then_inc(s_out, 16)
            sp.wait_ge(s_out, 16)

        @block.gpsimd
        def _(pool):
            pool.memset(ident[:, :], 0.0).then_inc(s_ident, 1)
            pool.memset(ones[:, :], 1.0).then_inc(s_ident, 1)
            pool.wait_ge(s_ident, 2)
            pool.affine_select(out=ident[:, :], in_=ident[:, :], compare_op=ALU.not_equal, fill=1.0, base=0,
                               pattern=[[-1, P]], channel_multiplier=1).then_inc(s_ident, 1)
            pool.wait_ge(s_ids, 16)
            for t in range(BT):
                for f in range(F):
                    slot, _ = group(t, f // GF)
                    if f % GF == 0:
                        n = FG * t + f // GF
                        if n == FG:
                            pool.wait_ge(s_g, 1)
                        if n >= GR:
                            pool.wait_ge(s_df, GF * (n - GR + 1) + DR)
                    at = f % GF * E
                    pool.indirect_dma_start(stream[:, slot, at:at + E], None, a[f"tbl_{f}"],
                                            bass.IndirectOffsetOnAxis(ids[:, t, f:f + 1], 0)).then_inc(s_gat[slot], 16)
            with pool.Fori(0, ROUNDS) as r:
                for s in range(2):
                    pool.wait_ge(s_wh, 2 * r + s + 1)
                    pool.tensor_tensor(w7l[:, s, :], raw[:, s, :], w7h[:, s, :].bitcast(F32), ALU.subtract)\
                        .then_inc(s_wl, 1)

        @block.vector
        def _(dve):
            dve.memset(padrow[:, :], PAD).then_inc(s_jf, JR)
            dve.wait_ge(s_v, 32)
            dve.tensor_tensor(vi, vi, vj, ALU.mult).then_inc(s_gp, 1)
            dve.wait_ge(s_gp, 1)
            dve.tensor_reduce(g[:, :], vi, AX.X, ALU.add).then_inc(s_g, 1)
            dve.wait_ge(s_wsp, 1)
            for n in range(2):
                dve.tensor_copy(wsc[:, n, :], acc[:, n, 0:E + 1]).then_inc(s_wsc, 1)
            dve.wait_ge(s_wsc, 2)

            def score(t, grp, i, j):
                slot, _ = group(t, grp)
                f = DR * i + j
                for s in range(2):
                    dve.wait_ge(s_jf, scored(t) + 2 * (GF * grp + f) + s + 1)
                    dve.scalar_tensor_tensor(junk[:, s, :], stream[:, slot, bass.ds(f * E, E)], 1.0,
                                             wsc[:, s, 0:E], ALU.mult, ALU.mult,
                                             accum_out=sa[:, s, bass.ds(GF * grp + f, 1)]).then_inc(s_jf, 1)

            def softmax(t):
                dve.wait_ge(s_ab, t + 1)
                dve.tensor_scalar(padded[:, :], absum[:, :], 0.0, None, ALU.is_equal).then_inc(s_ms, 1)
                dve.wait_ge(s_ms, 4 * t + 1)
                dve.wait_ge(s_e1, 2 * (t + 1))
                for s in range(2):
                    dve.copy_predicated(es[:, s, :], padded[:, :], padrow[:, :]).then_inc(s_ms, 1)
                dve.wait_ge(s_ms, 4 * t + 3)
                dve.tensor_reduce(nmax[:, :], es[:, :, :], AX.X, ALU.max).then_inc(s_ms, 1)
                dve.wait_ge(s_ms, 4 * t + 4)
                dve.tensor_scalar(nmax[:, :], nmax[:, :], -1.0, None, ALU.mult).then_inc(s_mx, 1)
                dve.wait_ge(s_p, 2 * (t + 1))
                dve.reciprocal(rden[:, t % 2, :], psum_[:, :]).then_inc(s_rd, 1)

            for t in range(-1, BT):
                for grp in range(FG):
                    if t + 1 < BT:
                        slot, count = group(t + 1, grp)
                        dve.wait_ge(s_gat[slot], count)
                    if t < 0:
                        with dve.Fori(0, 2) as i:
                            for j in range(DR):
                                score(0, grp, i, j)
                        continue
                    if t == 0:
                        dve.wait_ge(s_ident, 3)
                    with dve.Fori(0, 2) as i:
                        for j in range(DR):
                            f = GF * grp + DR * i + j
                            dve.wait_ge(s_df, F * t + f + 1)
                            dve.tensor_scalar(diag[:, j, 0, :], ident[:, :], pr[:, t % 2, 0, bass.ds(f, 1)], None,
                                              ALU.mult).then_inc(s_d[0], 1)
                            if t + 1 < BT:
                                score(t + 1, grp, i, j)
                if t + 1 < BT:
                    softmax(t + 1)

            def product(r, d):
                dve.tensor_tensor(cross[:, :, d * E:(d + 1) * E], hh[:, :, 0:E],
                                  hh[:, :, bass.ds(DG * r + d + 1, E)], ALU.mult).then_inc(s_cr, 1)

            def low(r, k, rows):
                n = TR * r + k
                dve.wait_ge(s_ch_, n + 1)
                dve.scalar_tensor_tensor(crossTl[0:rows, k % CR, :], xp[0:rows, k % XB, :], g[0:rows, bass.ds(n, 1)],
                                         crossTh[0:rows, k % CR, :].bitcast(F32), ALU.mult, ALU.subtract)\
                   .then_inc(s_cl, 1)

            def round_(r, tiles, rows_last, more):
                for k in range(tiles):
                    low(r, k, TP if k + 1 < tiles else rows_last)
                    for d in range(DG):
                        if more and k == min((E * (d + 1) - 1) // TP, TR - 1):
                            dve.wait_ge(s_xt, TR * r + k + 1)
                            product(r + 1, d)

            dve.wait_ge(s_tp, (STEPS - 1) * (BT - 1) + 4)
            for d in range(DG):
                product(0, d)
            with dve.Fori(0, ROUNDS - 1) as r:
                round_(r, TR, TP, True)
            round_(ROUNDS - 1, TLAST, PLAST, False)

            with dve.Fori(0, BT // 2) as h:
                for c in range(2 * LC):
                    if c % LC == 0:
                        t = 2 * h + c // LC
                        dve.wait_ge(s_o8, t + 1)
                        dve.wait_ge(s_zt, t + 1)
                        dve.tensor_tensor(o8[:, :], po8[:, 0:E], o6[:, bass.ds(t, 1), :].rearrange("p t e -> p (t e)"),
                                          ALU.add).then_inc(s_o8t, 1)
                        dve.wait_ge(s_o8t, t + 1)
                    dve.wait_ge(s_lab[c % LR], 16 * (2 * LC // LR * h + c // LR + 1))
                    for k in range(LK):
                        sl = stream[:, c % LR, k * E:(k + 1) * E]
                        col = c % LC * LK + k
                        ins = dve.tensor_tensor_reduce(sl, sl, o8[:, :], 1.0, 0.0, ALU.mult, ALU.add,
                                                       z[:, col:col + 1])
                    ins.then_inc(s_lu, 1)

        @block.scalar
        def _(act):
            act.wait_ge(s_wsc, 2)

            def absum_of(t, grp, i, j):
                slot, _ = group(t, grp)
                f = DR * i + j
                act.wait_ge(s_ajf, F * t + GF * grp + f + 1)
                act.activation(ajunk, stream[:, slot, bass.ds(f * E, E)], ACT.Abs,
                               accum_out=absum[:, bass.ds(GF * grp + f, 1)]).then_inc(s_ajf, 1)

            def softmax(t):
                act.wait_ge(s_ajf, F * (t + 1) + 1)
                act.nop().then_inc(s_ab, 1)
                act.wait_ge(s_jf, scored(t + 1) + JR)
                for s in range(2):
                    act.activation(es[:, s, :], sa[:, s, :], ACT.Exp, bias=wsc[:, s, E:E + 1]).then_inc(s_e1, 1)
                act.wait_ge(s_mx, t + 1)
                for s in range(2):
                    act.activation(pr[:, t % 2, s, :], es[:, s, :], ACT.Exp, bias=nmax[:, s:s + 1],
                                   accum_out=psum_[:, s:s + 1]).then_inc(s_p, 1)
                act.wait_ge(s_p, 2 * (t + 1))

            def chunks(ap):
                return ap.rearrange("p (c b) -> p c b", b=P)

            def tail(t, n):
                if n:
                    act.wait_ge(s_tp, (STEPS - 1) * t + n)
                if n == 0:
                    act.wait_ge(s_pool, t + 1)
                    act.wait_ge(s_rd, t + 1)
                    for s in range(2):
                        ins = act.activation(q_sb[:, s, :], acc[:, 2 * (t % 2) + s, 0:E], ACT.Copy,
                                             scale=rden[:, t % 2, s:s + 1])
                elif n == 1:
                    for s in range(2):
                        ins = act.activation(qT[:, EC * s:EC * (s + 1), :], chunks(xp[0:ECH, s, 0:EC * P]), ACT.Copy)
                elif n == 2:
                    act.activation(hh[:, t, 0:E], xp[:, 2, 0:E], ACT.Copy)
                    ins = act.activation(hh[:, t, E:HW], xp[:, 2, 0:HW - E], ACT.Copy)
                elif n == 3:
                    ins = act.activation(hT, chunks(xp[0:ECH, 0, 0:EC * P]), ACT.Copy)
                elif n == 4:
                    ins = act.activation(f6s, xp[:, 1, 0:E], ACT.Copy)
                elif n == 5:
                    ins = act.activation(f6T, chunks(xp[0:ECH, 0, 0:EC * P]), ACT.Copy)
                elif n == 6:
                    ins = act.activation(o6[:, t, :], xp[:, 2, 0:E], ACT.Copy)
                ins.then_inc(s_te, 1)

            for t in range(-1, BT):
                if t >= 1:
                    tail(t - 1, 0)
                for grp in range(FG):
                    if t + 1 < BT:
                        slot, count = group(t + 1, grp)
                        act.wait_ge(s_gat[slot], count)
                        if t >= 0:
                            act.wait_ge(s_ms, 4 * (t + 1))
                    with act.Fori(0, 2) as i:
                        for j in range(DR):
                            f = GF * grp + DR * i + j
                            if t >= 0:
                                act.wait_ge(s_df, F * t + f + 1)
                                act.wait_ge(s_ident, 3)
                                act.activation(diag[:, j, 1, :], ident[:, :], ACT.Copy,
                                               scale=pr[:, t % 2, 1, bass.ds(f, 1)]).then_inc(s_d[1], 1)
                            if t + 1 < BT:
                                absum_of(t + 1, grp, i, j)
                    if t >= 1:
                        tail(t - 1, grp + 1)
                if t >= 1:
                    tail(t - 1, FG + 1)
                if t + 1 < BT:
                    softmax(t + 1)
            for n in range(STEPS):
                tail(BT - 1, n)

            def high(r, s):
                act.wait_ge(s_raw[s], 16 * (r + 1))
                if not isinstance(r, int):
                    act.wait_ge(s_cf, TR * r + TH * (s - 1) + CR)
                act.activation(w7h[:, s, :], raw[:, s, :], ACT.Copy).then_inc(s_wh, 1)

            def evacuate(r, k, rows):
                n = TR * r + k
                act.wait_ge(s_xt, n + 1)
                act.wait_ge(s_cf, n + 1)
                act.activation(crossTh[0:rows, k % CR, :], xp[0:rows, k % XB, :], ACT.Copy,
                               scale=g[0:rows, bass.ds(n, 1)]).then_inc(s_ch_, 1)

            def round_(r, tiles, rows_last, more):
                for k in range(tiles):
                    evacuate(r, k, TP if k + 1 < tiles else rows_last)
                    if k == 2 and not (isinstance(r, int) and r == 0):
                        high(r, 1)
                    if k == 8 and more:
                        high(r + 1, 0)

            act.wait_ge(s_g, 1)
            high(0, 0)
            high(0, 1)
            round_(0, TR, TP, False)
            act.wait_ge(s_raw[0], 32)
            act.wait_ge(s_cf, TR - TH + CR)
            act.activation(w7h[:, 0, :], raw[:, 0, :], ACT.Copy).then_inc(s_wh, 1)
            with act.Fori(1, ROUNDS - 1) as r:
                round_(r, TR, TP, True)
            act.wait_ge(s_raw[1], 16 * ROUNDS)
            act.wait_ge(s_cf, TR * (ROUNDS - 1) + CR)
            act.activation(w7h[:, 1, :], raw[:, 1, :], ACT.Copy).then_inc(s_wh, 1)
            for k in range(TLAST):
                evacuate(ROUNDS - 1, k, TP if k + 1 < TLAST else PLAST)

            def chain(t):
                act.activation(f7s, acc[:, bass.ds(t, 1), 0:E].rearrange("p t e -> p (t e)"), ACT.Copy).then_inc(s_che, 1)
                act.wait_ge(s_ch, t + 1)
                act.activation(f7T, chunks(xp[0:ECH, 0, 0:EC * P]), ACT.Copy).then_inc(s_che, 1)

            def tower(t):
                act.wait_ge(s_ml, 4 * t + 1)
                act.activation(zT, chunks(xp[0:KZ, 0, 0:2 * P]), ACT.Copy).then_inc(s_mle, 1)
                act.wait_ge(s_top, 16 * 7)
                act.wait_ge(s_ml, 4 * t + 2)
                for m in range(4):
                    ins = act.activation(h1T[:, m, :], xp[:, 1, m * P:(m + 1) * P], ACT.Relu, bias=bt1[:, m:m + 1])
                ins.then_inc(s_mle, 1)
                act.wait_ge(s_ml, 4 * t + 3)
                for m in range(2):
                    ins = act.activation(h2T[:, m, :], xp[:, 2, m * P:(m + 1) * P], ACT.Relu, bias=bt2[:, m:m + 1])
                ins.then_inc(s_mle, 1)
                act.wait_ge(s_ml, 4 * t + 4)
                act.activation(y_sb[:, bass.ds(t * P, P)], xp[0:1, 0, 0:P], ACT.Copy).then_inc(s_mle, 1)

            act.wait_ge(s_cf, TR * (ROUNDS - 1) + TLAST + CR)
            chain(0)
            with act.Fori(0, BT - 1) as t:
                act.wait_ge(s_o8, t + 1)
                chain(t + 1)
                tower(t)
            tower(BT - 1)

        @block.tensor
        def _(pe):
            pe.wait_ge(s_pre, 32)
            for n in range(2):
                ins = pe.matmul(acc[:, n, 0:E + 1], w12[:, n, :], wsw[:, n, :], start=True, stop=True)
            ins.then_inc(s_wsp, 1)
            pe.wait_ge(s_ident, 3)
            pe.wait_ge(s_wa, 16 * 7)
            pe.wait_ge(s_wsc, 2)
            pe.nop().then_inc(s_df, DR)
            pe.nop().then_inc(s_cf, CR)
            pe.nop().then_inc(s_ajf, 1)
            pe.nop().then_inc(s_zt, 1)

            def weighted(t, grp, i, j, start, stop):
                slot, _ = group(t, grp)
                f = DR * i + j
                for s in range(2):
                    pe.wait_ge(s_d[s], F * t + GF * grp + f + 1)
                    ins = pe.matmul(acc[:, 2 * (t % 2) + s, 0:E], diag[:, j, s, :], stream[:, slot, bass.ds(f * E, E)],
                                    start=start, stop=stop, skip_group_check=True)
                ins.then_inc(s_df, 1)

            def tail(t, n):
                pe.wait_ge(s_te, STEPS * t + n)
                if n == 1:
                    for s in range(2):
                        for c in range(EC):
                            ins = pe.transpose(xp[0:ECH, s, c * P:(c + 1) * P], q_sb[:, s, c * ECH:(c + 1) * ECH],
                                               ident[:, :])
                elif n in (3, 5):
                    src = hh[:, t, :] if n == 3 else f6s
                    for c in range(EC):
                        ins = pe.transpose(xp[0:ECH, 0, c * P:(c + 1) * P], src[:, c * ECH:(c + 1) * ECH], ident[:, :])
                else:
                    bank, row, left, right = {2: (2, 0, qT, w5), 4: (1, 1, hT, w6), 6: (2, 3, f6T, w8)}[n]
                    count = 2 * EC if n == 2 else EC
                    pe.matmul(xp[:, bank, 0:E], ones[:, :], brow[:, row, :], start=True, stop=False)
                    for c in range(count):
                        ins = pe.matmul(xp[:, bank, 0:E], left[:, c, :], right[:, c, :], start=False,
                                        stop=c == count - 1)
                ins.then_inc(s_tp, 1)

            for t in range(BT):
                for grp in range(FG):
                    slot, count = group(t, grp)
                    pe.wait_ge(s_gat[slot], count)
                    if grp in (0, FG - 1):
                        for f in range(GF):
                            weighted(t, grp, f // DR, f % DR, grp == 0 and f == 0, grp > 0 and f == GF - 1)
                    else:
                        with pe.Fori(0, 2) as i:
                            for j in range(DR):
                                weighted(t, grp, i, j, False, False)
                    if t >= 1:
                        tail(t - 1, grp + 1)
                pe.wait_ge(s_df, F * (t + 1) + DR)
                pe.nop().then_inc(s_pool, 1)
                if t >= 1:
                    tail(t - 1, STEPS - 1)
            for n in range(1, STEPS):
                tail(BT - 1, n)
            pe.wait_ge(s_te, STEPS * BT)

            for t in range(BT):
                pe.matmul(acc[:, t, 0:E], ones[:, :], brow[:, 2, :], start=True, stop=False, skip_group_check=True)

            def transpose(r, k, rows):
                hi = (TP * k + rows - 1) // E
                if k == 0 or hi > (TP * k - 1) // E:
                    pe.wait_ge(s_cr, DG * r + hi + 1)
                for t in range(BT):
                    ins = pe.transpose(xp[0:rows, k % XB, t * P:(t + 1) * P], cross[:, t, TP * k:TP * k + rows], ident[:, :])
                ins.then_inc(s_xt, 1)

            def multiply(r, k, rows, last=False):
                if k % TH == 0:
                    pe.wait_ge(s_wl, 2 * r + k // TH + 1)
                pe.wait_ge(s_cl, TR * r + k + 1)
                s, cols = k // TH, slice(k % TH * E, (k % TH + 1) * E)
                for t in range(BT):
                    bs = slice(t * P, (t + 1) * P)
                    for left, right in ((crossTh, w7h), (crossTh, w7l), (crossTl, w7h)):
                        ins = pe.matmul(acc[:, t, 0:E], left[0:rows, k % CR, bs], right[0:rows, s, cols],
                                        start=False, stop=last and left is crossTl, skip_group_check=True)
                ins.then_inc(s_cf, 1)

            transpose(0, 0, TP)
            transpose(0, 1, TP)
            with pe.Fori(0, ROUNDS - 1) as r:
                for k in range(TR):
                    transpose(r + (k + 2) // TR, (k + 2) % TR, TP)
                    multiply(r, k, TP)
            for k in range(TLAST):
                if k + 2 < TLAST:
                    transpose(ROUNDS - 1, k + 2, TP if k + 3 < TLAST else PLAST)
                multiply(ROUNDS - 1, k, TP if k + 1 < TLAST else PLAST, last=k + 1 == TLAST)

            def chain(t):
                pe.wait_ge(s_che, 2 * t + 1)
                for c in range(EC):
                    ins = pe.transpose(xp[0:ECH, 0, c * P:(c + 1) * P], f7s[:, c * ECH:(c + 1) * ECH], ident[:, :])
                ins.then_inc(s_ch, 1)
                pe.wait_ge(s_che, 2 * t + 2)
                if not isinstance(t, int):
                    pe.wait_ge(s_o8t, t)
                for c in range(EC):
                    ins = pe.matmul(po8[:, 0:E], f7T[:, c, :], w8[:, EC + c, :], start=c == 0, stop=c == EC - 1)
                ins.then_inc(s_o8, 1)

            def tower(t):
                pe.wait_ge(s_lu, LC * (t + 1))
                for c in range(2):
                    ins = pe.transpose(xp[0:KZ, 0, c * P:(c + 1) * P], z[:, c * KZ:(c + 1) * KZ], ident[:, :])
                ins.then_inc(s_ml, 1)
                pe.wait_ge(s_ml, 4 * t + 1)
                pe.nop().then_inc(s_zt, 1)
                pe.wait_ge(s_mle, 4 * t + 1)
                pe.wait_ge(s_top, 16 * 7)
                for m in range(4):
                    ms = slice(m * P, (m + 1) * P)
                    for c in range(2):
                        pe.matmul(xp[:, 1, ms], wt1[:, c, ms], zT[:, c, :], start=c == 0, stop=False)
                    ins = pe.matmul(xp[:, 1, ms], wt1c[:, ms], ctxT[:, bass.ds(t * P, P)], start=False, stop=True)
                ins.then_inc(s_ml, 1)
                pe.wait_ge(s_mle, 4 * t + 2)
                for m in range(2):
                    for c in range(4):
                        ins = pe.matmul(xp[:, 2, m * P:(m + 1) * P], wt2[:, c, m * P:(m + 1) * P], h1T[:, c, :],
                                        start=c == 0, stop=c == 3)
                ins.then_inc(s_ml, 1)
                pe.wait_ge(s_mle, 4 * t + 3)
                for c in range(2):
                    ins = pe.matmul(xp[0:1, 0, 0:P], wt3[:, c:c + 1], h2T[:, c, :], start=c == 0, stop=c == 1)
                ins.then_inc(s_ml, 1)
                pe.wait_ge(s_mle, 4 * t + 4)

            chain(0)
            with pe.Fori(0, BT - 1) as t:
                chain(t + 1)
                tower(t)
            tower(BT - 1)


def layout(inputs):
    f = {k: np.ascontiguousarray(v) for k, v in inputs.items()}
    i, j, there = pair_order()
    lo, hi = np.minimum(i, j), np.maximum(i, j)
    row = np.where(there, lo * (2 * E - 1 - lo) // 2 + hi - lo - 1, PAIRS)
    grid = np.full((ROUNDS, TR, P), PAIRS)
    grid[:, :, 0:TP] = row.reshape(ROUNDS, TR, TP)
    w7 = np.concatenate([f["L0_rec_w7"], np.zeros((1, E), np.float32)])
    d = {f"tbl_{n}": f[f"tbl_{n}"] for n in range(F)}
    halves = grid.reshape(ROUNDS, 2, TH, P).transpose(0, 1, 3, 2)
    d["w7"] = w7[halves].reshape(ROUNDS, 2, P, TH * E)
    v = np.concatenate([f["L0_rec_v"], np.zeros((1, C), np.float32)])
    for name, n in (("vi", i), ("vj", j)):
        at = np.full((ROUNDS, TR, P), E)
        at[:, :, 0:TP] = np.where(there, n, E).reshape(ROUNDS, TR, TP)
        d[name] = np.ascontiguousarray(v[at.reshape(ROUNDS * TR, P).T])
    d["ids"] = f["ids"]
    d["w13"] = np.stack([np.concatenate([f[f"L0_rec_w{n}"].T, f[f"L0_rec_b{n}"][:, None]], 1) for n in (1, 3)], 1)
    d["w24"] = np.stack([np.repeat(f[f"L0_rec_w{n}"], P, 1) for n in (2, 4)], 1)
    for n in (5, 6, 8):
        d[f"w{n}"] = f[f"L0_rec_w{n}"]
    for n in (5, 6, 7, 8):
        d[f"b{n}"] = f[f"L0_rec_b{n}"]
    d["lab"] = f["r_label_embedding"].reshape(BT, P, LC, LK * E).transpose(0, 2, 1, 3).reshape(BT * LC, P, LK * E)
    d["wt1"], d["wt2"] = f["W_top1"], f["W_top2"]
    d["wt3"] = np.ascontiguousarray(f["W_top3"].reshape(2, P).T)
    d["bt1"] = np.ascontiguousarray(f["b_top1"].reshape(4, P).T)
    d["bt2"] = np.ascontiguousarray(f["b_top2"].reshape(2, P).T)
    d["ctxT"] = np.ascontiguousarray(f["dense_ctx"].T)
    return {k: np.ascontiguousarray(x) for k, x in d.items()}


def kernel(**inputs):
    import concourse.bacc as bacc
    from concourse.bass_utils import run_bass_kernel_spmd

    nc = bacc.Bacc("TRN2", target_bir_lowering=False, num_devices=1)
    arrays = layout({k: np.asarray(v) for k, v in inputs.items()})
    aps = {k: nc.dram_tensor(f"in_{k}", v.shape, mybir.dt.from_np(v.dtype), kind="ExternalInput").ap()
           for k, v in arrays.items()}
    out = nc.dram_tensor("out_y", (B, 1), F32, kind="ExternalOutput").ap()
    build(nc, aps, out)
    r = run_bass_kernel_spmd(nc, [{f"in_{k}": v for k, v in arrays.items()}], core_ids=[0])
    return r.results[0]["out_y"]
```

```python
from contextlib import ExitStack

import numpy as np

import concourse.bass as bass
from concourse import mybir

F32 = mybir.dt.float32
F32R = mybir.dt.float32r
I32 = mybir.dt.int32
ALU = mybir.AluOpType
ACT = mybir.ActivationFunctionType
AX = mybir.AxisListType

P = 128
B, F, E, K = 512, 50, 300, 200
T = 8
C = 4
BT = B // P
EC, ECH = 3, E // 3
CTX, H1, H2 = 16, 512, 256
KZ = K // 2
PAD = float(np.float32(-2 ** 32 + 1))

PAIRS = E * (E - 1) // 2
DG, TP = 5, 125
MIX = 2 * TP
MR = (E - MIX) // 2
TR = 2 + 2 * DG
ROUNDS = E // 2 // DG
LOADED = (0, 1, 2, DG, DG + 1, DG + 2, TR - 1)
TLAST = TR - 1
HD = E + E // 2
REP = HD - MIX
assert MR * DG == TP and ROUNDS * DG * 2 == E

TH = TR // 2
GF = 10
FG = F // GF
FO = F // 2
GR = 8
DR = 5
JR = 2
XB = 4
CR = 4
LK = 10
LR = 10
LC = K // LK
LP = 2
assert TR % XB == 0 and TR % CR == 0 and LC == 2 * LR and LK == GF == 2 * DR and F == 2 * FO and FO == DR * FG


def block(k):
    if DG <= k < DG + 2:
        return k - DG, None
    return (2, k) if k < DG else (3, (k - 1 - DG) % DG)


def pair_order():
    p = np.arange(TP)
    blocks = [block(k) for k in range(TR)]
    row = np.stack([MIX + MR * n + p // DG if n < 2 else TP * (n - 2) + p for n, _ in blocks])
    shift = np.stack([p % DG if n < 2 else 0 * p + a for n, a in blocks])
    step = DG * (1 + np.arange(ROUNDS))[:, None, None]
    i, j, n = (row + shift) + 0 * step, row + step, row + 0 * step
    there = (step - shift < E // 2) | (n < TP) | (n >= E - (E // 2 - TP))
    return i % E, j % E, there


def build(nc, a, out):
    with ExitStack() as ctx:
        def sb(name, shape, dt=F32):
            return ctx.enter_context(nc.sbuf_tensor(name, shape, dt))

        def pb(name, shape):
            return ctx.enter_context(nc.psum_tensor(name, shape, F32))

        def sem(name):
            return ctx.enter_context(nc.semaphore(name))

        stream = sb("stream", [P, GR, GF * E])
        vi, vj = (stream[:, FG, n * ROUNDS * TR * C:(n + 1) * ROUNDS * TR * C]
                  .rearrange("p (n c) -> p n c", c=C) for n in range(2))
        raw = sb("raw", [P, 2, TH * E])
        w7h = sb("w7h", [P, 2, TH * E], F32R)
        w7l = sb("w7l", [P, 2, TH * E], F32R)
        q_sb = raw[:, 1, 0:2 * E].rearrange("p (a e) -> p a e", a=2)
        h_sb = q_sb[:, 0, :]
        qTh, qTl = (w[0:ECH, 1, 0:2 * EC * P].rearrange("p (c b) -> p c b", c=2 * EC) for w in (w7h, w7l))
        w12 = raw[0:T, 1, 0:2 * P].rearrange("p (a n) -> p a n", a=2)
        wsw = raw[0:T, 1, 2 * P:2 * P + 2 * (E + 1)].rearrange("p (a n) -> p a n", a=2)
        second = sb("second", [P, 4, B])
        flat2 = second[:, :, :].rearrange("p t n -> p (t n)")
        first = sb("first", [P, TR, B])
        flat = first[:, :, :].rearrange("p t n -> p (t n)")
        taken = [0]

        def part(n):
            taken[0] += n
            assert taken[0] <= TR * B
            return slice(taken[0] - n, taken[0])

        diag = flat[:, part(DR * 2 * P)].rearrange("p (r a n) -> p r a n", r=DR, a=2)
        wsc = flat[:, part(2 * (E + 1))].rearrange("p (a n) -> p a n", a=2)
        junk = flat[:, part(JR * E)].rearrange("p (r e) -> p r e", r=JR)
        own = flat[:, part(2 * E)].rearrange("p (s e) -> p s e", s=2)
        w5 = flat[0:ECH, part(2 * EC * E)].rearrange("p (c e) -> p c e", c=2 * EC)
        w6T = flat2[0:ECH, 0:EC * E].rearrange("p (c e) -> p c e", c=EC)
        b6 = flat2[0:ECH, EC * E:EC * E + EC]
        taken[0] = LK * E
        wt1 = flat2[0:KZ, 0:2 * H1].rearrange("p (c n) -> p c n", c=2)
        wt1c, ctxT = flat2[0:CTX, 2 * H1:3 * H1], flat2[0:CTX, 3 * H1:3 * H1 + B]
        wt2 = flat[:, part(4 * H2)].rearrange("p (c n) -> p c n", c=4)
        wt3, bt1, bt2 = flat[:, part(2)], flat[:, part(4)], flat[:, part(2)]
        zT = flat[0:KZ, part(2 * P)].rearrange("p (c b) -> p c b", c=2)
        h12 = flat[:, part(6 * P)]
        h1T = h12[:, 0:4 * P].rearrange("p (c b) -> p c b", c=4)
        h2T = h12[:, 4 * P:6 * P].rearrange("p (c b) -> p c b", c=2)
        z, o8 = flat[:, part(K)], flat[:, part(E)]
        f7s = h12[:, 0:E]
        f7T = h12[0:ECH, E:E + EC * P].rearrange("p (c b) -> p c b", c=EC)
        crossh = sb("crossh", [P, CR, B], F32R)
        crossl = sb("crossl", [P, CR, B], F32R)
        w5h, w5l = (w[0:ECH, :, :].rearrange("p r b -> p (r b)")[:, 0:2 * EC * E].rearrange("p (c e) -> p c e", c=2 * EC)
                    for w in (crossh, crossl))
        w8 = sb("w8", [ECH, 2 * EC, E])
        hT = sb("hT", [ECH, EC, B])
        g = sb("g", [P, ROUNDS * TR])
        ident = sb("ident", [P, P])
        brow = sb("brow", [1, 3, E])
        y_sb = brow[0:1, 0:2, :].rearrange("p n e -> p (n e)")[:, 0:B]
        ones = sb("ones", [1, P])
        ids = sb("ids", [P, BT, F], I32)
        sa = sb("sa", [P, 2, F])
        es = sb("es", [P, 2, F])
        pr = sb("pr", [P, 2, 2, F])
        absum = sb("absum", [P, F])
        padded = sb("padded", [P, F], I32)
        padrow = sb("padrow", [P, F])
        nmax = sb("nmax", [P, 2])
        psum_ = sb("psum_", [P, 2])
        rden = sb("rden", [P, 2, 2])

        acc = pb("acc", [P, BT, 512])
        xp = pb("xp", [P, XB, 512])
        o8p = xp[:, XB - 1, 0:E]
        ajunk = o8p

        s_ids = sem("ids_loaded")
        s_pre = sem("pool_weights_loaded")
        s_v = sem("v_loaded")
        s_wa = sem("w5_w6_w8_loaded")
        s_top = sem("top_weights_loaded")
        s_gat = [sem(f"gathered_{n}") for n in range(GR)]
        s_one = [sem(f"field_gathered_{n}") for n in range(GF)]
        s_raw = [sem(f"w7_loaded_{s}") for s in range(2)]
        s_wh = sem("w7_high_ready")
        s_wl = sem("w7_low_ready")
        s_lab = [sem(f"labels_loaded_{s}") for s in range(LR)]
        s_ident = sem("ident_ready")
        s_wsp = sem("score_weights_summed")
        s_wsc = sem("score_weights_ready")
        s_g = sem("g_ready")
        s_gp = sem("g_product_ready")
        s_jf = sem("junk_free")
        s_ajf = sem("act_junk_free")
        s_df = sem("diag_free")
        s_e1 = sem("score_exp_ready")
        s_ab = sem("abs_ready")
        s_ms = sem("mask_steps")
        s_mx = sem("max_ready")
        s_p = sem("softmax_exp_ready")
        s_rd = sem("rden_ready")
        s_d = [sem("diag1_ready"), sem("diag2_ready")]
        s_own = sem("vector_sums")
        s_pool = sem("pools_summed")
        s_te = sem("tail_evacuated")
        s_w5 = sem("w5_parts_ready")
        s_qh = sem("q_high_ready")
        s_ql = sem("q_low_ready")
        s_fo = sem("folded_weights_ready")
        s_fe = sem("folded_weights_evacuated")
        s_tp = sem("tail_products")
        s_hp = sem("h_written")
        s_hc = sem("h_copies_written")
        s_fi = {k: sem(f"first_factors_loaded_{k}") for k in LOADED}
        s_se = [sem(f"second_factors_loaded_{n}") for n in range(4)]
        s_cr = sem("cross_ready")
        s_crh = sem("cross_high_ready")
        s_cl = sem("cross_low_ready")
        s_cf = sem("cross_free")
        s_f7 = sem("f7_summed")
        s_ch = sem("chain_products")
        s_che = sem("chain_evacuated")
        s_o8 = sem("o8_summed")
        s_o8t = sem("o8_taken")
        s_lu = sem("vector_labels_used")
        s_lp = sem("label_products")
        s_la = sem("label_products_summed")
        s_zt = sem("z_taken")
        s_ml = sem("tower_products")
        s_mle = sem("tower_evacuated")
        s_out = sem("out_written")

        h_plain = nc.dram_tensor("h_plain", (HD, B), F32, kind="Internal").ap()
        h_copies = nc.dram_tensor("h_copies", (REP, DG, B), F32, kind="Internal").ap()

        engines = ctx.enter_context(nc.Block())

        def chunks(ap):
            return ap.rearrange("p (c b) -> p c b", b=P)

        def labels(n):
            if n < GR:
                return stream[:, n, :]
            return (raw[:, :, :].rearrange("p s n -> p (s n)") if n == GR else flat)[:, 0:LK * E]

        def scored(t):
            return 2 * F * t

        def group(t, n):
            n = FG * t + n
            return n % GR, 16 * GF * (n // GR + 1 - sum(m <= n and m % GR == n % GR for m in (FG - 1, 2 * FG - 1)))

        HWRITES = 3
        STEPS = 3
        TSTEPS = 5
        TOPS = 7
        CHUNKS = BT * LC
        TOGETHER = 3
        AHEAD = 2

        @engines.sync
        def _(sp):
            sp.dma_start(ids[:, :, :], a["ids"].rearrange("(t p) f -> p t f", p=P)).then_inc(s_ids, 16)
            sp.dma_start(w12, a["w24"]).then_inc(s_pre, 16)
            sp.dma_start(wsw, a["w13"]).then_inc(s_pre, 16)
            sp.dma_start(vi, a["vi"]).then_inc(s_v, 16)
            sp.dma_start(vj, a["vj"]).then_inc(s_v, 16)
            sp.dma_start(w5, a["w5"].rearrange("(c p) e -> p c e", p=ECH)).then_inc(s_wa, 16)
            sp.dma_start(w6T, a["w6T"].rearrange("(c p) e -> p c e", p=ECH)).then_inc(s_wa, 16)
            sp.dma_start(b6, a["b6"]).then_inc(s_wa, 16)
            sp.dma_start(w8[:, :, :], a["w8"].rearrange("(c p) e -> p c e", p=ECH)).then_inc(s_wa, 16)
            for n, name in enumerate(("b5", "b7", "b8")):
                sp.dma_start(brow[0:1, n, :], a[name].rearrange("(o e) -> o e", o=1)).then_inc(s_wa, 16)
            sp.dma_start(raw[:, 0, :], a["w7"][0, 0]).then_inc(s_raw[0], 16)

            def copies(ap):
                return ap.unsqueeze(1).broadcast_to([ap.shape[0], DG, ap.shape[1]])

            for t in range(BT):
                bs = slice(t * P, (t + 1) * P)
                sp.wait_ge(s_te, STEPS * (t + 1))
                sp.dma_start(h_plain[0:E, bs].rearrange("(c p) b -> p c b", p=ECH), hT[:, :, bs]).then_inc(s_hp, 16)
                sp.dma_start(h_plain[E:E + ECH, bs], hT[:, 0, bs]).then_inc(s_hp, 16)
                sp.dma_start(h_plain[E + ECH:HD, bs], hT[0:HD - E - ECH, 1, bs]).then_inc(s_hp, 16)
                at = E - MIX
                sp.dma_start(h_copies[0:at, :, bs], copies(hT[ECH - at:ECH, 2, bs])).then_inc(s_hc, 16)
                sp.dma_start(h_copies[at:at + ECH, :, bs], copies(hT[:, 0, bs])).then_inc(s_hc, 16)
                sp.dma_start(h_copies[at + ECH:REP, :, bs], copies(hT[0:REP - at - ECH, 1, bs])).then_inc(s_hc, 16)

            def second_factors(r, n):
                if n < 2:
                    src = h_copies[bass.ds(DG * r + DG + MR * n, MR), :, :].rearrange("r a b -> (r a) b")
                else:
                    src = h_plain[bass.ds(DG * r + DG + TP * (n - 2), TP), :]
                sp.dma_start(second[0:TP, n, :], src).then_inc(s_se[n], 16)

            def first_factors(k, count=1):
                n, shift = block(k)
                if n < 2:
                    src = bass.AP(h_plain.tensor, (MIX + MR * n) * B, [[B, MR], [B, DG], [1, B]])
                    sp.dma_start(first[0:TP, k, :], src).then_inc(s_fi[k], 16)
                else:
                    src = bass.AP(h_plain.tensor, (TP * (n - 2) + shift) * B, [[B, TP], [B, count], [1, B]])
                    sp.dma_start(first[0:TP, k:k + count, :], src).then_inc(s_fi[k], 16)

            sp.wait_ge(s_hp, 16 * HWRITES * BT)
            second_factors(0, 2)
            first_factors(0)
            first_factors(1)
            first_factors(2, DG - 2)
            sp.dma_start(raw[:, 1, :], a["w7"][0, 1]).then_inc(s_raw[1], 16)
            sp.wait_ge(s_hc, 16 * HWRITES * BT)
            for n in range(2):
                first_factors(DG + n)
                second_factors(0, n)
            second_factors(0, 3)
            first_factors(2 + DG, DG - 1)
            first_factors(TR - 1)

            def w7_half(r, s):
                sp.wait_ge(s_wl, 2 * r + s - 1)
                src = a["w7"][r, s] if isinstance(r, int) else a["w7"][bass.ds(r, 1), s, :, :].rearrange("r p n -> (r p) n")
                sp.dma_start(raw[:, s, :], src).then_inc(s_raw[s], 16)

            def round_loads(r, more):
                sp.wait_ge(s_cr, TR * (r - 1) + DG)
                second_factors(r, 2)
                w7_half(r, 1)
                sp.wait_ge(s_cr, TR * (r - 1) + DG + 2)
                second_factors(r, 0)
                second_factors(r, 1)
                if more:
                    w7_half(r + 1, 0)
                sp.wait_ge(s_cr, TR * r)
                second_factors(r, 3)

            w7_half(1, 0)
            for r in range(1, GR + 1):
                round_loads(r, True)
                sp.dma_start(labels(r - 1), a["lab"][r - 1]).then_inc(s_lab[r - 1], 16)
            with sp.Fori(GR + 1, ROUNDS - 1) as r:
                round_loads(r, True)
            round_loads(ROUNDS - 1, False)
            sp.wait_ge(s_wl, 2 * ROUNDS)
            sp.dma_start(labels(GR), a["lab"][GR]).then_inc(s_lab[GR], 16)
            sp.wait_ge(s_cr, TR * (ROUNDS - 1) + TLAST)
            sp.dma_start(wt1, a["wt1"][0:K, :].rearrange("(c p) n -> p c n", p=KZ)).then_inc(s_top, 16)
            sp.dma_start(wt1c, a["wt1"][K:K + CTX, :]).then_inc(s_top, 16)
            sp.dma_start(ctxT, a["ctxT"]).then_inc(s_top, 16)
            sp.dma_start(wt2, a["wt2"].rearrange("(c p) n -> p c n", p=P)).then_inc(s_top, 16)
            sp.dma_start(wt3, a["wt3"]).then_inc(s_top, 16)
            sp.dma_start(bt1, a["bt1"]).then_inc(s_top, 16)
            sp.dma_start(bt2, a["bt2"]).then_inc(s_top, 16)
            sp.dma_start(labels(GR + 1), a["lab"][GR + 1]).then_inc(s_lab[GR + 1], 16)
            with sp.Fori(1, CHUNKS // LR) as r:
                for s in range(LR):
                    sp.wait_ge(s_lu, LR * (r - 1) + s + 1)
                    sp.wait_ge(s_la, LR * (r - 1) + s + 1)
                    sp.dma_start(labels(s), a["lab"][bass.ds(LR * r + s, 1), :, :].rearrange("c p n -> (c p) n"))\
                      .then_inc(s_lab[s], 16)
            sp.wait_ge(s_mle, TSTEPS * BT)
            sp.dma_start(out.rearrange("b o -> o b"), y_sb).then_inc(s_out, 16)
            sp.wait_ge(s_out, 16)

        @engines.gpsimd
        def _(pool):
            pool.memset(ident[:, :], 0.0).then_inc(s_ident, 1)
            pool.memset(ones[:, :], 1.0).then_inc(s_ident, 1)
            pool.wait_ge(s_ident, 2)
            pool.affine_select(out=ident[:, :], in_=ident[:, :], compare_op=ALU.not_equal, fill=1.0, base=0,
                               pattern=[[-1, P]], channel_multiplier=1).then_inc(s_ident, 1)
            pool.wait_ge(s_ids, 16)
            for t in range(BT):
                for f in range(F):
                    slot, _ = group(t, f // GF)
                    if f % GF == 0:
                        n = FG * t + f // GF
                        if n == FG:
                            pool.wait_ge(s_g, 1)
                        if n >= GR:
                            pool.wait_ge(s_df, GF * (n - GR + 1) + DR)
                    at = f % GF * E
                    pool.indirect_dma_start(stream[:, slot, at:at + E], None, a[f"tbl_{f}"],
                                            bass.IndirectOffsetOnAxis(ids[:, t, f:f + 1], 0))\
                        .then_inc(s_one[f % GF] if t < 2 and f >= F - GF else s_gat[slot], 16)
            with pool.Fori(0, ROUNDS) as r:
                for s in range(2):
                    pool.wait_ge(s_wh, 2 * r + s + 1)
                    for n in range(0, TH, 2):
                        at = slice(n * E, (n + 2) * E)
                        ins = pool.tensor_tensor(w7l[:, s, at], raw[:, s, at], w7h[:, s, at].bitcast(F32), ALU.subtract)
                    ins.then_inc(s_wl, 1)
            with pool.Fori(0, BT) as t:
                pool.wait_ge(s_o8t, 2 * t + 2)
                for c in range(LC):
                    pool.wait_ge(s_lab[c % LR], 16 * (LC // LR * t + c // LR + 1))
                    for k in range(LK - LP, LK):
                        sl = labels(c % LR)[:, k * E:(k + 1) * E]
                        ins = pool.tensor_tensor(sl, sl, o8, ALU.mult)
                    ins.then_inc(s_lp, 1)

        @engines.vector
        def _(dve):
            dve.memset(padrow[:, :], PAD).then_inc(s_jf, JR)
            dve.memset(own, 0.0).then_inc(s_own, 2)
            dve.wait_ge(s_v, 32)
            dve.tensor_tensor(vi, vi, vj, ALU.mult).then_inc(s_gp, 1)
            dve.wait_ge(s_gp, 1)
            dve.tensor_reduce(g[:, :], vi, AX.X, ALU.add).then_inc(s_g, 1)
            dve.wait_ge(s_wsp, 1)
            for n in range(2):
                dve.tensor_copy(wsc[:, n, :], acc[:, n, 0:E + 1]).then_inc(s_wsc, 1)
            dve.wait_ge(s_wsc, 2)
            dve.wait_ge(s_w5, 1)
            dve.tensor_tensor(w5l, w5, w5h.bitcast(F32), ALU.subtract).then_inc(s_w5, 1)

            def score(t, grp, i, j):
                slot, _ = group(t, grp)
                f = DR * i + j
                for s in range(2):
                    dve.wait_ge(s_jf, scored(t) + 2 * (GF * grp + f) + s + 1)
                    dve.scalar_tensor_tensor(junk[:, s, :], stream[:, slot, bass.ds(f * E, E)], 1.0,
                                             wsc[:, s, 0:E], ALU.mult, ALU.mult,
                                             accum_out=sa[:, s, bass.ds(GF * grp + f, 1)]).then_inc(s_jf, 1)

            def maximum(t):
                dve.wait_ge(s_ab, t + 1)
                dve.tensor_scalar(padded[:, :], absum[:, :], 0.0, None, ALU.is_equal).then_inc(s_ms, 1)
                dve.wait_ge(s_ms, 4 * t + 1)
                dve.wait_ge(s_e1, 2 * (t + 1))
                for s in range(2):
                    dve.copy_predicated(es[:, s, :], padded[:, :], padrow[:, :]).then_inc(s_ms, 1)
                dve.wait_ge(s_ms, 4 * t + 3)
                dve.tensor_reduce(nmax[:, :], es[:, :, :], AX.X, ALU.max).then_inc(s_ms, 1)
                dve.wait_ge(s_ms, 4 * t + 4)
                dve.tensor_scalar(nmax[:, :], nmax[:, :], -1.0, None, ALU.mult).then_inc(s_mx, 1)

            def q_low(t):
                for s in range(2):
                    dve.wait_ge(s_qh, 2 * t + s + 1)
                    cs = slice(EC * s, EC * (s + 1))
                    ins = dve.tensor_tensor(qTl[:, cs, :], chunks(xp[0:ECH, s, 0:EC * P]), qTh[:, cs, :].bitcast(F32),
                                            ALU.subtract)
                ins.then_inc(s_ql, 1)

            def denominator(t):
                dve.wait_ge(s_p, 2 * (t + 1))
                dve.reciprocal(rden[:, t % 2, :], psum_[:, :]).then_inc(s_rd, 1)

            for grp in range(FG - 1):
                slot, count = group(0, grp)
                dve.wait_ge(s_gat[slot], count)
                with dve.Fori(0, 2) as i:
                    for j in range(DR):
                        score(0, grp, i, j)
            for f in range(GF):
                dve.wait_ge(s_one[f], 16)
                score(0, FG - 1, 0, f)
            maximum(0)
            denominator(0)
            dve.wait_ge(s_ident, 3)

            def first_diag(t, grp, i, j):
                f = GF * grp + DR * i + j
                dve.wait_ge(s_df, F * t + f + 1)
                dve.tensor_scalar(diag[:, j % DR, 0, :], ident[:, :], pr[:, t % 2, 0, bass.ds(f, 1)], None,
                                  ALU.mult).then_inc(s_d[0], 1)

            for t in range(BT - 1):
                for grp in range(FG):
                    slot, count = group(t + 1, grp)
                    if t == 0 and grp == 0:
                        for f in range(DR):
                            first_diag(0, 0, 0, f)
                    if t == 0 and grp == FG - 1:
                        for f in range(GF):
                            first_diag(0, grp, 0, f)
                            dve.wait_ge(s_one[f], 32)
                            score(1, grp, 0, f)
                        maximum(1)
                        denominator(1)
                        continue
                    dve.wait_ge(s_gat[slot], count)
                    if t == 0 and grp == 0:
                        for f in range(DR):
                            score(1, 0, 0, 2 * f)
                            score(1, 0, 0, 2 * f + 1)
                            first_diag(0, 0, 1, f)
                        continue
                    if t >= 1 and grp == 2:
                        q_low(t - 1)
                    if grp + 1 < FG:
                        with dve.Fori(0, 2) as i:
                            for j in range(DR):
                                first_diag(t, grp, i, j)
                                score(t + 1, grp, i, j)
                        continue
                    for f in range(GF):
                        first_diag(t, grp, f // DR, f % DR)
                        if f < DR:
                            score(t + 1, grp, 0, 2 * f)
                            score(t + 1, grp, 0, 2 * f + 1)
                        if f == DR:
                            maximum(t + 1)
                    denominator(t + 1)

            for i in range(FO // DR):
                if i == 2:
                    q_low(BT - 2)
                for j in range(DR):
                    first_diag(BT - 1, 0, i, j)
                    f = F - FO + DR * i + j
                    slot, _ = group(BT - 1, f // GF)
                    for s in range(2):
                        dve.wait_ge(s_own, 2 * (DR * i + j) + s + 1)
                        dve.scalar_tensor_tensor(own[:, s, :], stream[:, slot, f % GF * E:(f % GF + 1) * E],
                                                 pr[:, (BT - 1) % 2, s, f:f + 1], own[:, s, :], ALU.mult, ALU.add)\
                           .then_inc(s_own, 1)

            def cross(r, k):
                n, place = TR * r + k, block(k)[0]
                if isinstance(r, int) and r == 0 and k in LOADED:
                    dve.wait_ge(s_fi[k], 16)
                if k in (0, DG, DG + 1, DG + 2):
                    dve.wait_ge(s_se[place], 16 * (r + 1))
                if not (isinstance(r, int) and r == 0 and k < XB):
                    dve.wait_ge(s_cl, n - XB + 1)
                dve.scalar_tensor_tensor(xp[0:TP, k % XB, :], first[0:TP, k, :], g[0:TP, bass.ds(n, 1)],
                                         second[0:TP, place, :], ALU.mult, ALU.mult).then_inc(s_cr, 1)

            def low(r, k):
                n = TR * r + k
                dve.wait_ge(s_crh, n + 1)
                dve.tensor_tensor(crossl[0:TP, k % CR, :], xp[0:TP, k % XB, :], crossh[0:TP, k % CR, :].bitcast(F32),
                                  ALU.subtract).then_inc(s_cl, 1)

            q_low(BT - 1)
            dve.wait_ge(s_te, STEPS * BT)
            for k in range(TR):
                cross(0, k)
                if k == 0:
                    low(0, 0)
                elif k > AHEAD:
                    low(0, k - AHEAD)
            with dve.Fori(1, ROUNDS - 1) as r:
                for k in range(TR):
                    cross(r, k)
                    low(r if k >= AHEAD else r - 1, (k - AHEAD) % TR)
            for k in range(TLAST):
                cross(ROUNDS - 1, k)
                low(ROUNDS - 1 if k >= AHEAD else ROUNDS - 2, (k - AHEAD) % TR)
            for k in range(TLAST - AHEAD, TLAST):
                low(ROUNDS - 1, k)

            with dve.Fori(0, BT) as t:
                dve.wait_ge(s_o8, t + 1)
                dve.wait_ge(s_zt, t + 1)
                src = acc[:, bass.ds(t, 1), 0:E].rearrange("p t e -> p (t e)")
                dve.tensor_copy(o8, src).then_inc(s_o8t, 1)
                dve.tensor_copy(o8p, src).then_inc(s_o8t, 1)
                dve.wait_ge(s_o8t, 2 * t + 2)
                for c in range(LC):
                    dve.wait_ge(s_lab[c % LR], 16 * (LC // LR * t + c // LR + 1))
                    for k in range(LK - LP):
                        sl = labels(c % LR)[:, k * E:(k + 1) * E]
                        ins = dve.tensor_tensor_reduce(sl, sl, o8p, 1.0, 0.0, ALU.mult, ALU.add,
                                                       z[:, c * LK + k:c * LK + k + 1])
                    ins.then_inc(s_lu, 1)

        @engines.scalar
        def _(act):
            act.wait_ge(s_wa, 16 * 7)
            act.activation(w5h, w5, ACT.Copy).then_inc(s_w5, 1)
            act.wait_ge(s_fo, 1)
            for m in range(EC):
                act.activation(w8[:, m, :], xp[0:ECH, m, 0:E], ACT.Copy).then_inc(s_fe, 1)
            act.activation(brow[:, 2, :], acc[0:1, 3, 0:E], ACT.Copy).then_inc(s_fe, 1)
            act.wait_ge(s_wsc, 2)

            def absum_of(t, grp, i, j):
                slot, _ = group(t, grp)
                f = DR * i + j
                act.wait_ge(s_ajf, F * t + GF * grp + f + 1)
                act.activation(ajunk, stream[:, slot, bass.ds(f * E, E)], ACT.Abs,
                               accum_out=absum[:, bass.ds(GF * grp + f, 1)]).then_inc(s_ajf, 1)

            def exponentials(t):
                act.wait_ge(s_ajf, F * (t + 1) + 1)
                act.nop().then_inc(s_ab, 1)
                act.wait_ge(s_jf, scored(t + 1) + JR)
                for s in range(2):
                    act.activation(es[:, s, :], sa[:, s, :], ACT.Exp, bias=wsc[:, s, E:E + 1]).then_inc(s_e1, 1)

            def softmax(t):
                act.wait_ge(s_mx, t + 1)
                for s in range(2):
                    act.activation(pr[:, t % 2, s, :], es[:, s, :], ACT.Exp, bias=nmax[:, s:s + 1],
                                   accum_out=psum_[:, s:s + 1]).then_inc(s_p, 1)
                act.wait_ge(s_p, 2 * (t + 1))

            def tail(t, n):
                if n:
                    act.wait_ge(s_tp, STEPS * t + n)
                if n == 0:
                    act.wait_ge(s_pool, t + 1)
                    act.wait_ge(s_rd, t + 1)
                    for s in range(2):
                        ins = act.activation(q_sb[:, s, :], acc[:, 2 * (t % 2) + s, 0:E], ACT.Copy,
                                             scale=rden[:, t % 2, s:s + 1])
                elif n == 1:
                    for s in range(2):
                        act.activation(qTh[:, EC * s:EC * (s + 1), :], chunks(xp[0:ECH, s, 0:EC * P]), ACT.Copy)\
                           .then_inc(s_qh, 1)
                elif n == 2:
                    ins = act.activation(h_sb, xp[:, 2, 0:E], ACT.Copy)
                elif n == 3:
                    ins = act.activation(hT[:, :, t * P:(t + 1) * P], chunks(xp[0:ECH, 0, 0:EC * P]), ACT.Copy)
                if n != 1:
                    ins.then_inc(s_te, 1)

            def second_diag(t, grp, i, j):
                f = GF * grp + DR * i + j
                act.wait_ge(s_df, F * t + f + 1)
                act.activation(diag[:, j % DR, 1, :], ident[:, :], ACT.Copy,
                               scale=pr[:, t % 2, 1, bass.ds(f, 1)]).then_inc(s_d[1], 1)

            for grp in range(FG - 1):
                slot, count = group(0, grp)
                act.wait_ge(s_gat[slot], count)
                with act.Fori(0, 2) as i:
                    for j in range(DR):
                        absum_of(0, grp, i, j)
            for f in range(GF):
                act.wait_ge(s_one[f], 16)
                absum_of(0, FG - 1, 0, f)
            exponentials(0)
            softmax(0)
            act.wait_ge(s_ident, 3)
            for t in range(BT - 1):
                for grp in range(FG):
                    slot, count = group(t + 1, grp)
                    if t == 0 and grp == 0:
                        for f in range(DR):
                            second_diag(0, 0, 0, f)
                    if t == 0 and grp == FG - 1:
                        for f in range(GF):
                            second_diag(0, grp, 0, f)
                            act.wait_ge(s_one[f], 32)
                            absum_of(1, grp, 0, f)
                        exponentials(1)
                        softmax(1)
                        continue
                    act.wait_ge(s_gat[slot], count)
                    act.wait_ge(s_ms, 4 * (t + 1))
                    if t == 0 and grp == 0:
                        for f in range(DR):
                            absum_of(1, 0, 0, 2 * f)
                            absum_of(1, 0, 0, 2 * f + 1)
                            second_diag(0, 0, 1, f)
                        continue
                    if grp + 1 < FG:
                        with act.Fori(0, 2) as i:
                            for j in range(DR):
                                second_diag(t, grp, i, j)
                                absum_of(t + 1, grp, i, j)
                    else:
                        for f in range(GF):
                            if f == DR:
                                exponentials(t + 1)
                            if f == DR + 3:
                                softmax(t + 1)
                            second_diag(t, grp, f // DR, f % DR)
                            if f < DR:
                                absum_of(t + 1, grp, 0, 2 * f)
                                absum_of(t + 1, grp, 0, 2 * f + 1)
                    if t >= 1 and grp != 2:
                        tail(t - 1, grp if grp < 2 else grp - 1)
            for i in range(FO // DR):
                for j in range(DR):
                    second_diag(BT - 1, 0, i, j)
                if i != 2:
                    tail(BT - 2, i if i < 2 else i - 1)
            for n in range(4):
                tail(BT - 1, n)

            def high(r, s):
                act.wait_ge(s_raw[s], 16 * (r + 1))
                if not (isinstance(r, int) and r == 0):
                    act.wait_ge(s_cf, TR * r + TH * (s - 1) + CR)
                act.activation(w7h[:, s, :], raw[:, s, :], ACT.Copy).then_inc(s_wh, 1)

            def cross_high(r, k):
                n = TR * r + k
                act.wait_ge(s_cr, n + 1)
                act.wait_ge(s_cf, n + 1)
                act.activation(crossh[0:TP, k % CR, :], xp[0:TP, k % XB, :], ACT.Copy).then_inc(s_crh, 1)

            def round_(r, tiles, more):
                for k in range(tiles):
                    cross_high(r, k)
                    if k == 2:
                        high(r, 1)
                    if k == 8 and more:
                        high(r + 1, 0)

            high(0, 0)
            round_(0, TR, True)
            with act.Fori(1, ROUNDS - 1) as r:
                round_(r, TR, True)
            round_(ROUNDS - 1, TLAST, False)

            def chain(t):
                act.wait_ge(s_f7, t + 1)
                act.activation(f7s, acc[:, bass.ds(t, 1), 0:E].rearrange("p t e -> p (t e)"), ACT.Copy).then_inc(s_che, 1)
                act.wait_ge(s_ch, t + 1)
                act.activation(f7T, chunks(xp[0:ECH, 2, 0:EC * P]), ACT.Copy).then_inc(s_che, 1)

            def half(t, c):
                for n in range(c * LC // 2, (c + 1) * LC // 2):
                    act.wait_ge(s_lp, LC * t + n + 1)
                    for k in range(LK - LP, LK):
                        sl = labels(n % LR)[:, k * E:(k + 1) * E]
                        ins = act.activation(sl, sl, ACT.Copy, accum_out=z[:, n * LK + k:n * LK + k + 1])
                    ins.then_inc(s_la, 1)
                act.wait_ge(s_ml, TSTEPS * t + c + 1)
                act.activation(zT[:, c, :], xp[0:KZ, 0, c * P:(c + 1) * P], ACT.Copy).then_inc(s_mle, 1)

            def tile(t, more):
                half(t, 0)
                if more:
                    act.wait_ge(s_o8, t + 1)
                    chain(t + 1)
                half(t, 1)
                act.wait_ge(s_ml, TSTEPS * t + 3)
                for m in range(4):
                    ins = act.activation(h1T[:, m, :], xp[:, 1, m * P:(m + 1) * P], ACT.Relu, bias=bt1[:, m:m + 1])
                ins.then_inc(s_mle, 1)
                act.wait_ge(s_ml, TSTEPS * t + 4)
                for m in range(2):
                    ins = act.activation(h2T[:, m, :], xp[:, 2, m * P:(m + 1) * P], ACT.Relu, bias=bt2[:, m:m + 1])
                ins.then_inc(s_mle, 1)
                act.wait_ge(s_ml, TSTEPS * t + 5)
                act.activation(y_sb[:, bass.ds(t * P, P)], xp[0:1, 0, 2 * P:3 * P], ACT.Copy).then_inc(s_mle, 1)

            chain(0)
            act.wait_ge(s_top, 16 * TOPS)
            with act.Fori(0, BT - 1) as t:
                tile(t, True)
            tile(BT - 1, False)

        @engines.tensor
        def _(pe):
            pe.wait_ge(s_pre, 32)
            for n in range(2):
                ins = pe.matmul(acc[:, n, 0:E + 1], w12[:, n, :], wsw[:, n, :], start=True, stop=True)
            ins.then_inc(s_wsp, 1)
            pe.wait_ge(s_ident, 3)
            pe.wait_ge(s_wa, 16 * 7)
            for m in range(EC):
                for c in range(EC):
                    pe.matmul(xp[0:ECH, m, 0:E], w6T[:, c, m * ECH:(m + 1) * ECH], w8[:, c, :],
                              start=c == 0, stop=c == EC - 1)
            pe.matmul(acc[0:1, 3, 0:E], ones[:, 0:1], brow[:, 2, :], start=True, stop=False)
            for c in range(EC):
                ins = pe.matmul(acc[0:1, 3, 0:E], b6[:, c:c + 1], w8[:, c, :], start=False, stop=c == EC - 1)
            ins.then_inc(s_fo, 1)
            pe.wait_ge(s_fe, EC + 1)
            pe.wait_ge(s_w5, 2)
            pe.wait_ge(s_wsc, 2)
            pe.nop().then_inc(s_df, DR)
            pe.nop().then_inc(s_cf, CR)
            pe.nop().then_inc(s_ajf, 1)
            pe.nop().then_inc(s_zt, 1)

            def weighted(t, grp, i, j, start, stop):
                slot, _ = group(t, grp)
                f = DR * i + j
                for s in range(2):
                    pe.wait_ge(s_d[s], F * t + GF * grp + f + 1)
                    ins = pe.matmul(acc[:, 2 * (t % 2) + s, 0:E], diag[:, j, s, :], stream[:, slot, bass.ds(f * E, E)],
                                    start=start, stop=stop, skip_group_check=True)
                ins.then_inc(s_df, 1)

            def tail(t, n):
                if n == 1:
                    pe.wait_ge(s_te, STEPS * t + 1)
                    for s in range(2):
                        for c in range(EC):
                            ins = pe.transpose(xp[0:ECH, s, c * P:(c + 1) * P], q_sb[:, s, c * ECH:(c + 1) * ECH],
                                               ident[:, :])
                elif n == 2:
                    pe.wait_ge(s_qh, 2 * t + 2)
                    pe.wait_ge(s_ql, t + 1)
                    pe.matmul(xp[:, 2, 0:E], ones[:, :], brow[:, 0, :], start=True, stop=False)
                    for c in range(2 * EC):
                        for left, right in ((qTh, w5h), (qTh, w5l), (qTl, w5h)):
                            ins = pe.matmul(xp[:, 2, 0:E], left[:, c, :], right[:, c, :], start=False,
                                            stop=c == 2 * EC - 1 and left is qTl)
                else:
                    pe.wait_ge(s_te, STEPS * t + 2)
                    for c in range(EC):
                        ins = pe.transpose(xp[0:ECH, 0, c * P:(c + 1) * P], h_sb[:, c * ECH:(c + 1) * ECH], ident[:, :])
                ins.then_inc(s_tp, 1)

            for t in range(BT - 1):
                for grp in range(FG):
                    slot, count = group(t, grp)
                    if count:
                        pe.wait_ge(s_gat[slot], count)
                    if grp in (0, FG - 1):
                        for f in range(GF):
                            weighted(t, grp, f // DR, f % DR, grp == 0 and f == 0, grp > 0 and f == GF - 1)
                    else:
                        with pe.Fori(0, 2) as i:
                            for j in range(DR):
                                weighted(t, grp, i, j, False, False)
                    if t >= 1 and grp in (0, 2, 3):
                        tail(t - 1, 1 if grp == 0 else grp)
                pe.wait_ge(s_df, F * (t + 1) + DR)
                pe.nop().then_inc(s_pool, 1)
            for i in range(FO // DR):
                for j in range(DR):
                    weighted(BT - 1, i // 2, i % 2, j, i == j == 0, False)
                if i in (0, 2, 3):
                    tail(BT - 2, 1 if i == 0 else i)
            pe.wait_ge(s_own, 2 * FO + 2)
            for s in range(2):
                ins = pe.matmul(acc[:, 2 * ((BT - 1) % 2) + s, 0:E], ident[:, :], own[:, s, :], start=False, stop=True,
                                skip_group_check=True)
            ins.then_inc(s_pool, 1)
            for n in range(1, 4):
                tail(BT - 1, n)

            for t in range(BT):
                pe.matmul(acc[:, t, 0:E], ones[:, :], brow[:, 1, :], start=True, stop=False, skip_group_check=True)

            def products(t, k, last=False):
                s, cols, bs = k // TH, slice(k % TH * E, (k % TH + 1) * E), slice(t * P, (t + 1) * P)
                for left, right in ((crossh, w7h), (crossh, w7l), (crossl, w7h)):
                    ins = pe.matmul(acc[:, t, 0:E], left[0:TP, k % CR, bs], right[0:TP, s, cols],
                                    start=False, stop=last and left is crossl, skip_group_check=True)
                return ins

            def multiply(r, k):
                if k % TH == 0:
                    pe.wait_ge(s_wl, 2 * r + k // TH + 1)
                pe.wait_ge(s_cl, TR * r + k + 1)
                for t in range(BT):
                    ins = products(t, k)
                ins.then_inc(s_cf, 1)

            with pe.Fori(0, ROUNDS - 1) as r:
                for k in range(TR):
                    multiply(r, k)
            for k in range(TLAST - TOGETHER):
                multiply(ROUNDS - 1, k)

            def chain_transposes(t):
                pe.wait_ge(s_che, 2 * t + 1)
                for c in range(EC):
                    ins = pe.transpose(xp[0:ECH, 2, c * P:(c + 1) * P], f7s[:, c * ECH:(c + 1) * ECH], ident[:, :])
                ins.then_inc(s_ch, 1)

            def chain_products(t):
                pe.matmul(acc[:, t, 0:E], ones[:, :], brow[:, 2, :], start=True, stop=False, skip_group_check=True)
                for c in range(EC):
                    pe.matmul(acc[:, t, 0:E], hT[:, c, t * P:(t + 1) * P], w8[:, c, :], start=False, stop=False,
                              skip_group_check=True)
                pe.wait_ge(s_che, 2 * t + 2)
                for c in range(EC):
                    ins = pe.matmul(acc[:, t, 0:E], f7T[:, c, :], w8[:, EC + c, :], start=False, stop=c == EC - 1,
                                    skip_group_check=True)
                ins.then_inc(s_o8, 1)

            pe.wait_ge(s_cl, TR * (ROUNDS - 1) + TLAST)
            for t in range(BT):
                for k in range(TLAST - TOGETHER, TLAST):
                    ins = products(t, k, last=k + 1 == TLAST)
                ins.then_inc(s_f7, 1)
                if t == 1:
                    chain_transposes(0)
                    chain_products(0)

            def half(t, c):
                pe.wait_ge(s_lu, LC * t + (c + 1) * LC // 2)
                pe.wait_ge(s_la, LC * t + (c + 1) * LC // 2)
                pe.transpose(xp[0:KZ, 0, c * P:(c + 1) * P], z[:, c * KZ:(c + 1) * KZ], ident[:, :]).then_inc(s_ml, 1)
                if c == 0:
                    for m in range(4):
                        ms = slice(m * P, (m + 1) * P)
                        pe.matmul(xp[:, 1, ms], wt1c[:, ms], ctxT[:, t * P:(t + 1) * P], start=m == 0, stop=False,
                                  skip_group_check=True)
                else:
                    pe.wait_ge(s_ml, TSTEPS * t + 2)
                    pe.nop().then_inc(s_zt, 1)
                pe.wait_ge(s_mle, TSTEPS * t + c + 1)
                for m in range(4):
                    ms = slice(m * P, (m + 1) * P)
                    ins = pe.matmul(xp[:, 1, ms], wt1[:, c, ms], zT[:, c, :], start=False, stop=c == 1,
                                    skip_group_check=True)
                if c == 1:
                    ins.then_inc(s_ml, 1)

            pe.wait_ge(s_top, 16 * TOPS)
            for t in range(BT):
                half(t, 0)
                if t + 1 < BT:
                    chain_transposes(t + 1)
                    chain_products(t + 1)
                half(t, 1)
                pe.wait_ge(s_mle, TSTEPS * t + 3)
                for m in range(2):
                    for c in range(4):
                        ins = pe.matmul(xp[:, 2, m * P:(m + 1) * P], wt2[:, c, m * P:(m + 1) * P], h1T[:, c, :],
                                        start=c == 0, stop=c == 3)
                ins.then_inc(s_ml, 1)
                pe.wait_ge(s_mle, TSTEPS * t + 4)
                for c in range(2):
                    ins = pe.matmul(xp[0:1, 0, 2 * P:3 * P], wt3[:, c:c + 1], h2T[:, c, :], start=c == 0, stop=c == 1)
                ins.then_inc(s_ml, 1)
                pe.wait_ge(s_mle, TSTEPS * t + 5)


def layout(inputs):
    f = {k: np.ascontiguousarray(v) for k, v in inputs.items()}
    i, j, there = pair_order()
    lo, hi = np.minimum(i, j), np.maximum(i, j)
    grid = np.full((ROUNDS, TR, P), PAIRS)
    grid[:, :, 0:TP] = np.where(there, lo * (2 * E - 1 - lo) // 2 + hi - lo - 1, PAIRS)
    w7 = np.concatenate([f["L0_rec_w7"], np.zeros((1, E), np.float32)])
    d = {f"tbl_{n}": f[f"tbl_{n}"] for n in range(F)}
    halves = grid.reshape(ROUNDS, 2, TH, P).transpose(0, 1, 3, 2)
    d["w7"] = w7[halves].reshape(ROUNDS, 2, P, TH * E)
    v = np.concatenate([f["L0_rec_v"], np.zeros((1, C), np.float32)])
    for name, n in (("vi", i), ("vj", j)):
        at = np.full((ROUNDS, TR, P), E)
        at[:, :, 0:TP] = np.where(there, n, E)
        d[name] = np.ascontiguousarray(v[at.reshape(ROUNDS * TR, P).T])
    d["ids"] = f["ids"]
    d["w13"] = np.stack([np.concatenate([f[f"L0_rec_w{n}"].T, f[f"L0_rec_b{n}"][:, None]], 1) for n in (1, 3)], 1)
    d["w24"] = np.stack([np.repeat(f[f"L0_rec_w{n}"], P, 1) for n in (2, 4)], 1)
    d["w5"], d["w6T"], d["w8"] = f["L0_rec_w5"], f["L0_rec_w6"].T, f["L0_rec_w8"]
    d["b6"] = f["L0_rec_b6"].reshape(EC, ECH).T
    for n in (5, 7, 8):
        d[f"b{n}"] = f[f"L0_rec_b{n}"]
    d["lab"] = f["r_label_embedding"].reshape(BT, P, LC, LK * E).transpose(0, 2, 1, 3).reshape(BT * LC, P, LK * E)
    d["wt1"], d["wt2"] = f["W_top1"], f["W_top2"]
    d["wt3"] = np.ascontiguousarray(f["W_top3"].reshape(2, P).T)
    d["bt1"] = np.ascontiguousarray(f["b_top1"].reshape(4, P).T)
    d["bt2"] = np.ascontiguousarray(f["b_top2"].reshape(2, P).T)
    d["ctxT"] = np.ascontiguousarray(f["dense_ctx"].T)
    return {k: np.ascontiguousarray(x) for k, x in d.items()}


def kernel(**inputs):
    import concourse.bacc as bacc
    from concourse.bass_utils import run_bass_kernel_spmd

    nc = bacc.Bacc("TRN2", target_bir_lowering=False, num_devices=1)
    arrays = layout({k: np.asarray(v) for k, v in inputs.items()})
    aps = {k: nc.dram_tensor(f"in_{k}", v.shape, mybir.dt.from_np(v.dtype), kind="ExternalInput").ap()
           for k, v in arrays.items()}
    out = nc.dram_tensor("out_y", (B, 1), F32, kind="ExternalOutput").ap()
    build(nc, aps, out)
    r = run_bass_kernel_spmd(nc, [{f"in_{k}": v for k, v in arrays.items()}], core_ids=[0])
    return r.results[0]["out_y"]
```
